# Optimizing a Trainium2 kernel written in Bass

```python
import numpy as np
import jax
import jax.numpy as jnp

def _softmax(x, axis=-1):
    return jax.nn.softmax(x, axis=axis)

def _gelu(x):
    return jax.nn.gelu(x, approximate=True)

def _silu(x):
    return jax.nn.silu(x)

def _sigmoid(x):
    return jax.nn.sigmoid(x)

def _layernorm(x, axis=-1, eps=1e-05):
    m = jnp.mean(x, axis=axis, keepdims=True)
    v = jnp.var(x, axis=axis, keepdims=True)
    return (x - m) / jnp.sqrt(v + eps)

def _scatter_add(tgt, idx, src, axis=0):
    return tgt.at[idx].add(src)

def _segment_sum(src, seg, n):
    return jax.ops.segment_sum(src, seg, n)
kernel_name = 'mk_prb_d2_jaxref_r8_a19ec6'

def setup_inputs(seed: int=0):
    np.random.seed(seed)
    _w = jnp.asarray

    def _L0_attn_setup():
        import jax, jax.numpy as jnp
        import numpy as np
        BSZ, SEQ, DZ = (4, 256, 128)
        C, R = (16, 64)
        SCALE = 0.03125
        REG_H = 1.0
        key = jax.random.key(seed)
        k1, k2, k3 = jax.random.split(key, 3)
        qz = jax.random.normal(k1, (BSZ, SEQ, DZ), dtype=jnp.float32)
        ternary_factor_u = jax.random.normal(k2, (C * R, DZ), dtype=jnp.float32) * 0.02
        ternary_factor_v = jax.random.normal(k3, (C * R, DZ), dtype=jnp.float32) * 0.02
        return {'qz': qz, 'ternary_factor_u': ternary_factor_u, 'ternary_factor_v': ternary_factor_v}
    _L0_attn_in = _L0_attn_setup()

    def _L0_ffn_setup():
        import math
        import jax, jax.numpy as jnp
        import numpy as np
        E = 8
        H = 128
        HP = 128
        SPARSITY = 8
        N_ROTATE = 64
        ROPE_BASE = 10000.0

        def _rope(x, pos):
            half = N_ROTATE // 2
            inv_freq = 1.0 / ROPE_BASE ** (jnp.arange(half, dtype=jnp.float32) * 2.0 / N_ROTATE)
            ang = pos.astype(jnp.float32)[..., None] * inv_freq
            sin, cos = (jnp.sin(ang), jnp.cos(ang))
            x1, x2 = (x[..., :half], x[..., half:])
            return jnp.concatenate([x1 * cos - x2 * sin, x2 * cos + x1 * sin], axis=-1)
        key = jax.random.key(seed)
        k1, k2, k3, k4 = jax.random.split(key, 4)
        B, T = (4, 1024)
        X = jax.random.normal(k1, (B, T, H), dtype=jnp.float32)
        Wr = jax.random.uniform(k2, (E, H), minval=-1 / math.sqrt(H), maxval=1 / math.sqrt(H), dtype=jnp.float32)
        bq = 1 / math.sqrt(3 * HP)
        Wqkv = jax.random.uniform(k3, (E, H, 3 * HP), minval=-bq, maxval=bq, dtype=jnp.float32)
        bo = 1 / math.sqrt(H * E)
        Wo = jax.random.uniform(k4, (E, HP, H), minval=-bo, maxval=bo, dtype=jnp.float32)
        return {'X': X, 'Wr': Wr, 'Wqkv': Wqkv, 'Wo': Wo}
    _L0_ffn_in = _L0_ffn_setup()

    def _L1_attn_setup():
        import jax, jax.numpy as jnp
        import numpy as np
        D_MODEL = 128
        D_HEAD = 64
        RANK = 8
        LEAF = 4
        NUM_LEAVES = D_HEAD // LEAF
        NUM_LEVELS = 4
        BLOCK_SIZES = [4, 8, 16, 32]
        RANKS = [min(RANK, b) for b in BLOCK_SIZES]
        NUM_NODES = [NUM_LEAVES // 2 ** (l + 1) for l in range(NUM_LEVELS)]

        def _elu1(x):
            return jax.nn.elu(x) + 1.0

        def _hss_forward(x, Wq, Wk, Wv, Wo, UL, VR, UR, VL):
            B, T, _ = x.shape
            q = _elu1(x @ Wq)
            k = _elu1(x @ Wk)
            v = x @ Wv
            leaf0 = jnp.zeros((B, NUM_LEAVES, LEAF, LEAF), x.dtype)
            Ws0 = tuple((jnp.zeros((B, NUM_NODES[l], RANKS[l], RANKS[l]), x.dtype) for l in range(NUM_LEVELS)))
            z0 = jnp.zeros((B, D_HEAD), x.dtype)

            def step(carry, kvq):
                leaf, Ws, z = carry
                k_t, v_t, q_t = kvq
                leaf = leaf + jnp.einsum('bni,bnj->bnij', k_t.reshape(B, NUM_LEAVES, LEAF), v_t.reshape(B, NUM_LEAVES, LEAF))
                newWs = []
                for l in range(NUM_LEVELS):
                    bs, nn = (BLOCK_SIZES[l], NUM_NODES[l])
                    u_r = k_t.reshape(B, nn, 2 * bs)
                    v_r = v_t.reshape(B, nn, 2 * bs)
                    uL = jnp.einsum('bnd,dr->bnr', u_r[:, :, :bs], UL[l])
                    vR = jnp.einsum('bnd,dr->bnr', v_r[:, :, bs:], VR[l])
                    newWs.append(Ws[l] + jnp.einsum('bni,bnj->bnij', uL, vR))
                Ws = tuple(newWs)
                z = z + k_t
                y = jnp.einsum('bnij,bnj->bni', leaf, q_t.reshape(B, NUM_LEAVES, LEAF)).reshape(B, D_HEAD)
                for l in range(NUM_LEVELS):
                    bs, nn = (BLOCK_SIZES[l], NUM_NODES[l])
                    x_r = q_t.reshape(B, nn, 2 * bs)
                    vr_x = jnp.einsum('bnd,dr->bnr', x_r[:, :, bs:], VR[l])
                    y_top = jnp.einsum('dr,bnr->bnd', UL[l], jnp.einsum('bnij,bnj->bni', Ws[l], vr_x))
                    vl_x = jnp.einsum('bnd,dr->bnr', x_r[:, :, :bs], VL[l])
                    y_bot = jnp.einsum('dr,bnr->bnd', UR[l], jnp.einsum('bnji,bnj->bni', Ws[l], vl_x))
                    y = y + jnp.concatenate([y_top, y_bot], axis=-1).reshape(B, D_HEAD)
                denom = jnp.maximum(jnp.sum(z * q_t, axis=-1, keepdims=True), 1e-06)
                return ((leaf, Ws, z), y / denom)
            kvq = (jnp.swapaxes(k, 0, 1), jnp.swapaxes(v, 0, 1), jnp.swapaxes(q, 0, 1))
            _, outs = jax.lax.scan(step, (leaf0, Ws0, z0), kvq)
            out = jnp.swapaxes(outs, 0, 1)
            return out @ Wo
        key = jax.random.key(seed)
        ks = jax.random.split(key, 32)
        B, T = (8, 256)
        x = jax.random.normal(ks[0], (B, T, D_MODEL), jnp.float32)
        s_in = 1.0 / np.sqrt(D_MODEL)
        s_out = 1.0 / np.sqrt(D_HEAD)
        inp = {'x': x, 'Wq': jax.random.normal(ks[1], (D_MODEL, D_HEAD), jnp.float32) * s_in, 'Wk': jax.random.normal(ks[2], (D_MODEL, D_HEAD), jnp.float32) * s_in, 'Wv': jax.random.normal(ks[3], (D_MODEL, D_HEAD), jnp.float32) * s_in, 'Wo': jax.random.normal(ks[4], (D_HEAD, D_MODEL), jnp.float32) * s_out}
        idx = 5
        for name in ['UL', 'VR', 'UR', 'VL']:
            for l in range(NUM_LEVELS):
                bs, rl = (BLOCK_SIZES[l], RANKS[l])
                Q, _ = jnp.linalg.qr(jax.random.normal(ks[idx], (bs, rl), jnp.float32))
                inp[f'{name}{l}'] = Q
                idx += 1
        return inp
    _L1_attn_in = _L1_attn_setup()

    def _L1_ffn_setup():
        import jax, jax.numpy as jnp
        import numpy as np
        DIM = 128
        HIDDEN = 384
        SCALE = 1.0 / 127.0

        def _dequant(w_int, dtype):
            return w_int.astype(dtype) * jnp.asarray(SCALE, dtype)
        key = jax.random.key(seed)
        k_x, k_g, k_u, k_d = jax.random.split(key, 4)
        x = jax.random.normal(k_x, (4, 256, DIM), dtype=jnp.float32)
        w_gate = jax.random.randint(k_g, (HIDDEN, DIM), -127, 128, dtype=jnp.int32)
        w_up = jax.random.randint(k_u, (HIDDEN, DIM), -127, 128, dtype=jnp.int32)
        w_down = jax.random.randint(k_d, (DIM, HIDDEN), -127, 128, dtype=jnp.int32)
        return {'x': x, 'w_gate': w_gate, 'w_up': w_up, 'w_down': w_down}
    _L1_ffn_in = _L1_ffn_setup()
    _d = {'L0_attn_qz': _L0_attn_in['qz'], 'L0_attn_ternary_factor_u': _L0_attn_in['ternary_factor_u'], 'L0_attn_ternary_factor_v': _L0_attn_in['ternary_factor_v'], 'L0_ffn_Wr': _L0_ffn_in['Wr'], 'L0_ffn_Wqkv': _L0_ffn_in['Wqkv'], 'L0_ffn_Wo': _L0_ffn_in['Wo'], 'L1_attn_Wq': _L1_attn_in['Wq'], 'L1_attn_Wk': _L1_attn_in['Wk'], 'L1_attn_Wv': _L1_attn_in['Wv'], 'L1_attn_Wo': _L1_attn_in['Wo'], 'L1_attn_UL0': _L1_attn_in['UL0'], 'L1_attn_UL1': _L1_attn_in['UL1'], 'L1_attn_UL2': _L1_attn_in['UL2'], 'L1_attn_UL3': _L1_attn_in['UL3'], 'L1_attn_VR0': _L1_attn_in['VR0'], 'L1_attn_VR1': _L1_attn_in['VR1'], 'L1_attn_VR2': _L1_attn_in['VR2'], 'L1_attn_VR3': _L1_attn_in['VR3'], 'L1_attn_UR0': _L1_attn_in['UR0'], 'L1_attn_UR1': _L1_attn_in['UR1'], 'L1_attn_UR2': _L1_attn_in['UR2'], 'L1_attn_UR3': _L1_attn_in['UR3'], 'L1_attn_VL0': _L1_attn_in['VL0'], 'L1_attn_VL1': _L1_attn_in['VL1'], 'L1_attn_VL2': _L1_attn_in['VL2'], 'L1_attn_VL3': _L1_attn_in['VL3'], 'L1_ffn_w_gate': _L1_ffn_in['w_gate'], 'L1_ffn_w_up': _L1_ffn_in['w_up'], 'L1_ffn_w_down': _L1_ffn_in['w_down']}
    _x0 = _d['L0_attn_qz']
    _d['L0_attn_qz'] = jax.random.normal(jax.random.fold_in(jax.random.key(seed), 1), (8, 512, 128), dtype=_x0.dtype)
    del _x0
    return _d

def reference(L0_attn_qz, L0_attn_ternary_factor_u, L0_attn_ternary_factor_v, L0_ffn_Wr, L0_ffn_Wqkv, L0_ffn_Wo, L1_attn_Wq, L1_attn_Wk, L1_attn_Wv, L1_attn_Wo, L1_attn_UL0, L1_attn_UL1, L1_attn_UL2, L1_attn_UL3, L1_attn_VR0, L1_attn_VR1, L1_attn_VR2, L1_attn_VR3, L1_attn_UR0, L1_attn_UR1, L1_attn_UR2, L1_attn_UR3, L1_attn_VL0, L1_attn_VL1, L1_attn_VL2, L1_attn_VL3, L1_ffn_w_gate, L1_ffn_w_up, L1_ffn_w_down):

    def _L0_attn_ref(qz, ternary_factor_u, ternary_factor_v):
        import jax, jax.numpy as jnp
        import numpy as np
        BSZ, SEQ, DZ = (4, 256, 128)
        C, R = (16, 64)
        SCALE = 0.03125
        REG_H = 1.0
        bsz, seq_len, _ = qz.shape
        qz_u = qz @ ternary_factor_u.T * SCALE
        qz_v = qz @ ternary_factor_v.T * SCALE
        qz_u = qz_u.reshape(bsz, seq_len, C, R).transpose(0, 2, 1, 3)
        qz_v = qz_v.reshape(bsz, seq_len, C, R).transpose(0, 2, 1, 3)
        message_F = jnp.einsum('bcsr,bctr->bcst', qz_u, qz_v)
        qh = jax.nn.sigmoid(message_F / REG_H)
        qh_v1 = jnp.einsum('bcst,bctr->bcsr', qh, qz_v)
        qh_v2 = jnp.einsum('bcst,bcsr->bctr', qh, qz_u)
        qh_v1 = qh_v1.transpose(0, 2, 1, 3).reshape(bsz, seq_len, C * R)
        qh_v2 = qh_v2.transpose(0, 2, 1, 3).reshape(bsz, seq_len, C * R)
        message_G = (qh_v1 @ ternary_factor_u + qh_v2 @ ternary_factor_v) * SCALE
        return message_G

    def _L0_ffn_ref(X, Wr, Wqkv, Wo):
        import math
        import jax, jax.numpy as jnp
        import numpy as np
        E = 8
        H = 128
        HP = 128
        SPARSITY = 8
        N_ROTATE = 64
        ROPE_BASE = 10000.0

        def _rope(x, pos):
            half = N_ROTATE // 2
            inv_freq = 1.0 / ROPE_BASE ** (jnp.arange(half, dtype=jnp.float32) * 2.0 / N_ROTATE)
            ang = pos.astype(jnp.float32)[..., None] * inv_freq
            sin, cos = (jnp.sin(ang), jnp.cos(ang))
            x1, x2 = (x[..., :half], x[..., half:])
            return jnp.concatenate([x1 * cos - x2 * sin, x2 * cos + x1 * sin], axis=-1)
        B, T, _ = X.shape
        k = min(max(T // SPARSITY, 2), T)
        logits = jax.nn.sigmoid(jnp.einsum('bth,eh->bte', X, Wr))
        topk_vals, topk_I = jax.lax.top_k(logits.transpose(0, 2, 1), k)
        idx_flat = topk_I.reshape(B, E * k)
        Xg = jnp.take_along_axis(X, idx_flat[:, :, None], axis=1).reshape(B, E, k, H)
        QKV = jnp.einsum('beki,eij->bekj', Xg, Wqkv)
        Q, K, V = jnp.split(QKV, 3, axis=-1)
        Q = jnp.concatenate([_rope(Q[..., :N_ROTATE], topk_I), Q[..., N_ROTATE:]], axis=-1)
        K = jnp.concatenate([_rope(K[..., :N_ROTATE], topk_I), K[..., N_ROTATE:]], axis=-1)
        M = topk_I[..., :, None] >= topk_I[..., None, :]
        scores = jnp.einsum('bekd,bemd->bekm', Q, K) / math.sqrt(HP)
        scores = jnp.where(M, scores, -jnp.inf)
        A = jax.nn.softmax(scores, axis=-1)
        AV = jnp.einsum('bekm,bemd->bekd', A, V)
        AV = AV * topk_vals[..., None]
        Xpre = jnp.einsum('bekj,eji->beki', AV, Wo)
        out = jnp.zeros((B, T, H), dtype=X.dtype)
        out = out.at[jnp.arange(B)[:, None], idx_flat].add(Xpre.reshape(B, E * k, H))
        return out

    def _L1_attn_ref(x, Wq, Wk, Wv, Wo, UL0, UL1, UL2, UL3, VR0, VR1, VR2, VR3, UR0, UR1, UR2, UR3, VL0, VL1, VL2, VL3):
        import jax, jax.numpy as jnp
        import numpy as np
        D_MODEL = 128
        D_HEAD = 64
        RANK = 8
        LEAF = 4
        NUM_LEAVES = D_HEAD // LEAF
        NUM_LEVELS = 4
        BLOCK_SIZES = [4, 8, 16, 32]
        RANKS = [min(RANK, b) for b in BLOCK_SIZES]
        NUM_NODES = [NUM_LEAVES // 2 ** (l + 1) for l in range(NUM_LEVELS)]

        def _elu1(x):
            return jax.nn.elu(x) + 1.0

        def _hss_forward(x, Wq, Wk, Wv, Wo, UL, VR, UR, VL):
            B, T, _ = x.shape
            q = _elu1(x @ Wq)
            k = _elu1(x @ Wk)
            v = x @ Wv
            leaf0 = jnp.zeros((B, NUM_LEAVES, LEAF, LEAF), x.dtype)
            Ws0 = tuple((jnp.zeros((B, NUM_NODES[l], RANKS[l], RANKS[l]), x.dtype) for l in range(NUM_LEVELS)))
            z0 = jnp.zeros((B, D_HEAD), x.dtype)

            def step(carry, kvq):
                leaf, Ws, z = carry
                k_t, v_t, q_t = kvq
                leaf = leaf + jnp.einsum('bni,bnj->bnij', k_t.reshape(B, NUM_LEAVES, LEAF), v_t.reshape(B, NUM_LEAVES, LEAF))
                newWs = []
                for l in range(NUM_LEVELS):
                    bs, nn = (BLOCK_SIZES[l], NUM_NODES[l])
                    u_r = k_t.reshape(B, nn, 2 * bs)
                    v_r = v_t.reshape(B, nn, 2 * bs)
                    uL = jnp.einsum('bnd,dr->bnr', u_r[:, :, :bs], UL[l])
                    vR = jnp.einsum('bnd,dr->bnr', v_r[:, :, bs:], VR[l])
                    newWs.append(Ws[l] + jnp.einsum('bni,bnj->bnij', uL, vR))
                Ws = tuple(newWs)
                z = z + k_t
                y = jnp.einsum('bnij,bnj->bni', leaf, q_t.reshape(B, NUM_LEAVES, LEAF)).reshape(B, D_HEAD)
                for l in range(NUM_LEVELS):
                    bs, nn = (BLOCK_SIZES[l], NUM_NODES[l])
                    x_r = q_t.reshape(B, nn, 2 * bs)
                    vr_x = jnp.einsum('bnd,dr->bnr', x_r[:, :, bs:], VR[l])
                    y_top = jnp.einsum('dr,bnr->bnd', UL[l], jnp.einsum('bnij,bnj->bni', Ws[l], vr_x))
                    vl_x = jnp.einsum('bnd,dr->bnr', x_r[:, :, :bs], VL[l])
                    y_bot = jnp.einsum('dr,bnr->bnd', UR[l], jnp.einsum('bnji,bnj->bni', Ws[l], vl_x))
                    y = y + jnp.concatenate([y_top, y_bot], axis=-1).reshape(B, D_HEAD)
                denom = jnp.maximum(jnp.sum(z * q_t, axis=-1, keepdims=True), 1e-06)
                return ((leaf, Ws, z), y / denom)
            kvq = (jnp.swapaxes(k, 0, 1), jnp.swapaxes(v, 0, 1), jnp.swapaxes(q, 0, 1))
            _, outs = jax.lax.scan(step, (leaf0, Ws0, z0), kvq)
            out = jnp.swapaxes(outs, 0, 1)
            return out @ Wo
        UL = (UL0, UL1, UL2, UL3)
        VR = (VR0, VR1, VR2, VR3)
        UR = (UR0, UR1, UR2, UR3)
        VL = (VL0, VL1, VL2, VL3)
        return _hss_forward(x, Wq, Wk, Wv, Wo, UL, VR, UR, VL)

    def _L1_ffn_ref(x, w_gate, w_up, w_down):
        import jax, jax.numpy as jnp
        import numpy as np
        DIM = 128
        HIDDEN = 384
        SCALE = 1.0 / 127.0

        def _dequant(w_int, dtype):
            return w_int.astype(dtype) * jnp.asarray(SCALE, dtype)
        wg = _dequant(w_gate, x.dtype)
        wu = _dequant(w_up, x.dtype)
        wd = _dequant(w_down, x.dtype)
        gate = jnp.einsum('bsd,hd->bsh', x, wg)
        up = jnp.einsum('bsd,hd->bsh', x, wu)
        h = jax.nn.silu(gate) * up
        return jnp.einsum('bsh,dh->bsd', h, wd)
    x = L0_attn_qz
    xn = _layernorm(x, axis=-1)
    x = x + _L0_attn_ref(xn, L0_attn_ternary_factor_u, L0_attn_ternary_factor_v) + _L0_ffn_ref(xn, L0_ffn_Wr, L0_ffn_Wqkv, L0_ffn_Wo)
    xn = _layernorm(x, axis=-1)
    x = x + _L1_attn_ref(xn, L1_attn_Wq, L1_attn_Wk, L1_attn_Wv, L1_attn_Wo, L1_attn_UL0, L1_attn_UL1, L1_attn_UL2, L1_attn_UL3, L1_attn_VR0, L1_attn_VR1, L1_attn_VR2, L1_attn_VR3, L1_attn_UR0, L1_attn_UR1, L1_attn_UR2, L1_attn_UR3, L1_attn_VL0, L1_attn_VL1, L1_attn_VL2, L1_attn_VL3) + _L1_ffn_ref(xn, L1_ffn_w_gate, L1_ffn_w_up, L1_ffn_w_down)
    return x

_drawn_inputs = setup_inputs


def setup_inputs(seed=0):
    import zlib

    import numpy as np

    out = dict(_drawn_inputs(seed))
    spreads = {}
    factors = {'L0_attn_ternary_factor_u': 8.0,
     'L0_attn_ternary_factor_v': 8.0,
     'L1_attn_Wq': 8.0,
     'L1_attn_Wk': 8.0,
     'L1_attn_Wv': 8.0,
     'L1_attn_Wo': 8.0,
     'L1_attn_UL0': 8.0,
     'L1_attn_UL1': 8.0,
     'L1_attn_UL2': 8.0,
     'L1_attn_UL3': 8.0,
     'L1_attn_VR0': 8.0,
     'L1_attn_VR1': 8.0,
     'L1_attn_VR2': 8.0,
     'L1_attn_VR3': 8.0,
     'L1_attn_UR0': 8.0,
     'L1_attn_UR1': 8.0,
     'L1_attn_UR2': 8.0,
     'L1_attn_UR3': 8.0,
     'L1_attn_VL0': 8.0,
     'L1_attn_VL1': 8.0,
     'L1_attn_VL2': 8.0,
     'L1_attn_VL3': 8.0}
    for name, (base, spread) in spreads.items():
        noise = np.random.default_rng([zlib.crc32(name.encode()), seed]).standard_normal(out[name].shape)
        drawn = base * np.exp(spread * noise) if base else spread * noise
        out[name] = jnp.asarray(drawn.astype(out[name].dtype))
    for name, factor in factors.items():
        out[name] = (out[name] * factor).astype(out[name].dtype)
    return out
```

```python
from contextlib import ExitStack

import concourse.bass as bass
import numpy as np
from concourse import mybir

F32 = mybir.dt.float32
F32R = mybir.dt.float32r
I32 = mybir.dt.int32
ALU = mybir.AluOpType
ACT = mybir.ActivationFunctionType
AX = mybir.AxisListType

P = 128
B, T, D = 8, 512, 128
TB = T // P
EPS = 1e-5

C, R = 16, 64
PAIRS = C // 2
FACTOR_SCALE = 0.03125

E, KSEL = 8, 64
NROT = 64
EW = 3 * P + 2 * NROT + P
MASKED = -3.0e38

DH, LEAF = 64, 4
LEVELS = [(4, 4, 8), (8, 8, 4), (16, 8, 2), (32, 8, 1)]
NF = 7
ROUNDS = 6
HIDDEN = 384
HC = HIDDEN // P
W_SCALE = 1.0 / 127.0

UNITS = 2 * TB
F_BANKS = 3
TH_SLOTS = 4

L1_STEPS = [("norm", 0), ("k", 0), ("q", 0), ("v", 0)]
for _f in range(NF):
    L1_STEPS += [("B", _f), ("A", _f), ("C", _f)] + ([("D", _f)] if _f >= 2 else [])
L1_STEPS += [("den", 0)]
for _h in range(HC):
    L1_STEPS += [("gate", _h), ("up", _h)]
L1_STEPS += [("down", 0)]
NL = len(L1_STEPS)
STEP_AT = {s: n for n, s in enumerate(L1_STEPS)}
L1_FIRST_SLOT = 3


def round_of(kind, f):
    if f < 2:
        return 0, f
    return f - 1, 0 if kind == "C" else 1


def prep_index(g, k):
    return k - 1 if isinstance(g, int) and g < 0 else g * 5 + 3 + k


def build(nc, io):
    ctx = ExitStack()
    with ctx:
        def sb(name, shape, dt=F32):
            return ctx.enter_context(nc.sbuf_tensor(name, shape, dt))

        def sem(name):
            return ctx.enter_context(nc.semaphore(name))

        bank = [ctx.enter_context(nc.psum_tensor(f"bank{n}", [P, 512], F32)) for n in range(8)]
        f_bank = bank[0:F_BANKS]
        o_bank = bank[3:5]
        prep_bank, l1_bank, y_bank = bank[5], bank[6], bank[7]

        x_all = sb("x_all", [P, B, TB, D])
        xn1T = sb("xn1T", [P, B + 1, T])
        ident = sb("ident", [P, P])
        ones = sb("ones", [P, 512])
        uT_w, vT_w = sb("uT_w", [P, C * R]), sb("vT_w", [P, C * R])
        u_w, v_w = sb("u_w", [P, PAIRS, D]), sb("v_w", [P, PAIRS, D])
        kk_w, qq_w, vv_w = sb("kk_w", [P, P]), sb("qq_w", [P, P]), sb("vv_w", [P, P])
        wo2 = sb("wo2", [P, D])
        top_w, bot_w = sb("top_w", [P, ROUNDS, DH]), sb("bot_w", [P, ROUNDS, DH])
        zsel = sb("zsel", [P, 1])
        wg, wu = sb("wg", [P, HIDDEN]), sb("wu", [P, HIDDEN])
        wd = sb("wd", [P, HC, D])
        NA, NB_, ND = NF * P, NF * P, (NF - 2) * P
        e_str = sb("e_str", [P, NA + NB_ + ND], F32R)
        e_swp = sb("e_swp", [P, NA + NB_ + ND], F32R)
        E_AT = {"A": 0, "B": NA, "C": NA, "D": NA + NB_ - 2 * P}
        u_stk, v_stk, v_swp = (sb(n, [P, 2, 2, T], F32R) for n in ("u_stk", "v_stk", "v_swp"))
        k_stk, q_stk, vl_stk = (sb(n, [P, T], F32R) for n in ("k_stk", "q_stk", "vl_stk"))
        stats = sb("stats", [P, TB, 6])
        mv_s, rstd_s, ve = sb("mv_s", [P, TB, 2]), sb("rstd_s", [P, TB]), sb("ve", [P, TB])
        mr_s = sb("mr_s", [P, 2, TB])
        mean1, rstd1 = sb("mean1", [P, B, TB]), sb("rstd1", [P, B, TB])
        powc = sb("powc", [P, TB])
        idle = sb("idle", [P, 1])
        xn_s = sb("xn_s", [P, TB, D])
        sums = sb("sums", [P, 2, 2])
        small = sb("small", [P, 8])

        ARENA = 24000
        arena = sb("arena", [P, ARENA])
        at = [0]

        def take(*shape):
            n = int(np.prod(shape))
            a = arena[:, at[0]:at[0] + n]
            at[0] += n
            assert at[0] <= ARENA, at[0]
            if len(shape) == 2:
                return a.rearrange("p (a b) -> p a b", a=shape[0])
            if len(shape) == 3:
                return a.rearrange("p (a b c) -> p a b c", a=shape[0], b=shape[1])
            return a

        xgT = take(E, B, KSEL)
        csg = take(E, B, KSEL)
        y_all = take(B, E // 2, D)
        sel = take(TB, E * KSEL)
        rvT = take(2, TB, E * B)
        rk_s, vl_s = take(TB, E), take(TB, E)
        iota1 = take(KSEL)
        mark_scatter = at[0]
        table = take(TB, P)
        causal = take(P)
        we = take(2, EW)
        mark_experts = at[0]
        xg_s = take(T)
        t2q, t2k = take(T), take(T)
        qf, kf = take(T), take(T)
        v_s, s1, ptT, avT = take(TB, P), take(TB, P), take(TB, P), take(TB, P)
        y_s = take(2, TB, P)
        rmax, rsum, rinv = take(TB), take(TB), take(TB)
        at[0] = mark_experts
        wr_w = take(E)
        lg8 = take(B, T)
        lg = take(T)
        at[0] = mark_scatter
        sel_w = take(TB, E * KSEL)
        selT = take(E // 2, T)
        tk_val, tk_work, tk_mask, tk_pos, tk_rank = (xgT[0:E * B, e].rearrange("p b k -> p (b k)") for e in range(5))
        tk_m8 = small[0:E * B, 0:8]
        at[0] = 0
        e_raw = take(NA + NB_ + ND)
        wi = take(3 * HIDDEN).bitcast(I32)
        at[0] = 0
        u_raw, v_raw = take(T), take(T)
        u_tok, v_tok = take(2, TB, P), take(2, TB, P)
        th = take(TH_SLOTS, T)
        o_s = [take(2, T), take(2, T)]
        xn2T, kmin, kexp, kf32, bs, bs6, ab, pre = (take(T) for _ in range(8))
        pc = [take(2, T), take(2, T)]
        y_sb, tg, gated = take(T), take(T), take(T)
        hid = take(HC, T)

        s_stage, s_const, s_x = sem("stage_loaded"), sem("consts_loaded"), sem("x_loaded")
        s_prep_w, s_ones, s_powc = sem("weights_split"), sem("ones_set"), sem("powc_set")
        s_stats, s_ve, s_rstd = sem("stats_ready"), sem("var_eps_ready"), sem("rstd_ready")
        s_xn, s_xT, s_xnT = sem("xn_ready"), sem("xn_transposed"), sem("xn1T_ready")
        s_lg, s_lgc, s_lgd = sem("logits_done"), sem("logits_copied"), sem("logits_moved")
        s_ex, s_tk, s_tkT, s_rv = sem("router_exp"), sem("topk_done"), sem("topk_transposed"), sem("ranks_ready")
        s_sel, s_gath, s_gx = sem("sel_ready"), sem("gathered"), sem("gather_copied")
        s_we = [sem("expert_w0"), sem("expert_w1")]
        s_q3, s_rope, s_vd, s_vs = sem("qkr_done"), sem("rope_done"), sem("expert_v_done"), sem("expert_v_copied")
        s_sc, s_sm, s_pexp, s_pt, s_ptc = (sem(n) for n in ("scores_done", "shifted", "probs_ready", "probsT_done", "probsT_copied"))
        s_av, s_avc, s_yd, s_ys = (sem(n) for n in ("av_done", "av_copied", "expert_y_done", "expert_y_scaled"))
        s_ymv, s_ri = [sem("expert_y_moved0"), sem("expert_y_moved1")], sem("rinv_ready")
        s_qk_hi, s_xgs, s_gcs = sem("qk_passed_rows"), sem("picked_copied"), sem("angles_copied")
        s_selw, s_selT, s_selTc, s_scat, s_ffn = (sem(n) for n in ("selw_ready", "selT_done", "selT_copied", "scattered", "ffn_added"))
        s_chain = sem("dve_chain")
        s_prep_full, s_prep_free = sem("prep_bank_full"), sem("prep_bank_free")
        s_us, s_vs_rdy = sem("u_stack_ready"), sem("v_stack_ready")
        s_f, s_th, s_out, s_oe = sem("scores_full"), sem("tanh_done"), sem("unit_done"), sem("o_evacuated")
        s_lf, s_le = sem("l1_bank_full"), sem("l1_bank_free")
        s_stats2, s_ve2, s_rstd2, s_xn2 = sem("l1_stats"), sem("l1_var_eps"), sem("l1_rstd"), sem("l1_xn")
        s_min, s_exp, s_stk, s_tanh = sem("l1_min"), sem("l1_exp"), sem("l1_stack"), sem("l1_tanh")
        s_y, s_ysb, s_yo, s_yfree = sem("l1_y"), sem("l1_y_copied"), sem("l1_y_out"), sem("l1_y_bank_free")
        s_prd = sem("l1_prefix")
        s_st = sem("stored")
        s_hi = sem("split_hi")
        s_bs6 = sem("key_sum_ones")

        consts = [(ident, io["ident"]), (uT_w, io["uT"]), (vT_w, io["vT"]),
                  (u_w, io["u"].rearrange("(j p) d -> p j d", p=P)), (v_w, io["v"].rearrange("(j p) d -> p j d", p=P)),
                  (kk_w, io["wk2"]), (qq_w, io["wq2"]), (vv_w, io["wv2"]), (wo2, io["wo2"]),
                  (top_w, io["top"]), (bot_w, io["bot"]), (zsel, io["zsel"])]
        phase_consts = [(wr_w, io["wrT"]), (table, io["table"].rearrange("(k p) c -> p k c", p=P)),
                        (causal, io["causal"]), (iota1, io["iota1"])]
        wi_v = wi.rearrange("p (a b) -> p a b", a=3)

        block = ctx.enter_context(nc.Block())

        @block.sync
        def _(sp):
            sp.dma_start(x_all[:], io["x"].rearrange("b (k p) d -> p b k d", p=P)).then_inc(s_x, 16)
            for dst, src in consts + phase_consts:
                sp.dma_start(dst[:], src).then_inc(s_const, 16)
            sp.wait_ge(s_lgc, B)
            sp.dma_start(lg[0:E * B].rearrange("q t -> q t"), lg8[0:E].rearrange("e b t -> e b t")).then_inc(s_lgd, 16)
            for par in range(2):
                sp.dma_start(we[:, par], io["we"][par]).then_inc(s_we[par], 16)

            def move_rows(n, ep, par):
                sp.wait_ge(s_ys, n + 1)
                for half in range(2):
                    sp.dma_start(y_all[64 * par:64 * par + 64].rearrange("p (q r) e d -> p q r e d", r=2)[:, :, half, ep, :],
                                 y_s[64 * half:64 * half + 64, par]).then_inc(s_ymv[par], 16)

            with sp.Fori(0, E // 2 - 1) as ep:
                for par in range(2):
                    move_rows(ep * 2 + par, ep, par)
                    sp.wait_ge(s_yd, ep * 2 + par + 1)
                    sp.dma_start(we[:, par], io["we"][ep * 2 + par + 2]).then_inc(s_we[par], 16)
            for par in range(2):
                move_rows(E - 2 + par, E // 2 - 1, par)
            with sp.Fori(0, B) as n:
                sp.wait_ge(s_le, n * NL + NL)
                sp.dma_start(io["out"][n].rearrange("(k p) d -> p k d", p=P), x_all[:, n]).then_inc(s_st, 16)
            sp.wait_ge(s_st, 16 * B)

        @block.gpsimd
        def _(pool):
            pool.memset(powc[:], -0.5).then_inc(s_powc, 1)
            pool.memset(ones[:], 1.0).then_inc(s_ones, 1)
            pool.memset(xn1T[:, B, :], 0.0).then_inc(s_ones, 1)
            pool.dma_start(e_raw[:, 0:NA + NB_ + ND], io["e"]).then_inc(s_stage, 16)
            pool.dma_start(wi_v[:], io["wi"]).then_inc(s_stage, 16)
            pool.wait_ge(s_powc, 1)
            with pool.Fori(0, B) as n:
                pool.wait_ge(s_stats, n + 1)
                pool.tensor_tensor(rstd_s[:], ve[:], powc[:], ALU.pow).then_inc(s_rstd, 1)
            with pool.Fori(0, B) as n:
                pool.wait_ge(s_stats2, n + 1)
                pool.tensor_tensor(rstd_s[:], ve[:], powc[:], ALU.pow).then_inc(s_rstd2, 1)

        @block.vector
        def _(dve):
            chain = [0, 0]

            def link(ins):
                ins.then_inc(s_chain, 1)
                chain[1] += 1
                dve.wait_ge(s_chain, chain[0] + chain[1])

            def carry():
                nc.vector.memset(idle[:], 0.0)

            def loop(lo, hi, links, body):
                first = chain[0] + chain[1]
                with dve.Fori(lo, hi) as n:
                    chain[0], chain[1] = (n - lo if lo else n) * links + first, 0
                    body(n)
                    assert chain[1] == links, chain
                chain[0], chain[1] = first + (hi - lo) * links, 0

            dve.wait_ge(s_stage, 32)
            link(nc.vector.tensor_copy(e_str[:], e_raw[:]))
            nc.vector.tensor_copy(e_swp[64:128, :], e_raw[64:128, :])
            nc.vector.tensor_tensor(e_swp[0:64, :], e_raw[0:64, :], e_str[0:64, :], ALU.subtract)
            for lo, n in ((2 * P, NA), (NA + 2 * P, NA + NB_), (NA + NB_, NA + NB_ + ND)):
                nc.vector.tensor_tensor(e_str[64:128, lo:n], e_raw[64:128, lo:n], e_str[64:128, lo:n], ALU.subtract)
            nc.vector.tensor_scalar(wg[:], wi_v[:, 0], W_SCALE, None, ALU.mult)
            nc.vector.tensor_scalar(wu[:], wi_v[:, 1], W_SCALE, None, ALU.mult)
            nc.vector.tensor_scalar(wd[:], wi_v[:, 2].rearrange("p (h d) -> p h d", h=HC), W_SCALE, None, ALU.mult)\
              .then_inc(s_prep_w, 1)

            def statistics(n, done):
                carry()
                for k in range(TB):
                    ins = nc.vector.bn_stats(stats[:, k], x_all[:, n, k])
                link(ins)
                carry()
                for k in range(TB):
                    ins = nc.vector.bn_aggr(mv_s[:, k], stats[:, k])
                link(ins)
                nc.vector.tensor_scalar(ve[:], mv_s[:, :, 1], EPS, None, ALU.add).then_inc(done, 1)

            def normalised(n, mean, inv):
                for k in range(TB):
                    ins = nc.vector.tensor_scalar(xn_s[:, k], x_all[:, n, k], mean[:, k], inv[:, k],
                                                  ALU.subtract, ALU.mult)
                return ins

            dve.wait_ge(s_x, 16)

            def ln1(n):
                statistics(n, s_stats)
                dve.wait_ge(s_rstd, n + 1)
                dve.wait_ge(s_xT, n)
                normalised(n, mv_s[:, :, 0:1], rstd_s[:].unsqueeze(2)).then_inc(s_xn, 1)
                nc.vector.tensor_copy(mean1[:, n], mv_s[:, :, 0])
                link(nc.vector.tensor_copy(rstd1[:, n], rstd_s[:]))
            loop(0, B, 3, ln1)

            dve.wait_ge(s_ex, 1)
            link(nc.vector.tensor_scalar_add(tk_val, tk_work, 1.0))
            link(nc.vector.reciprocal(tk_val, tk_val))
            link(nc.vector.tensor_copy(tk_work, tk_val))

            def best8(n):
                link(nc.vector.max(tk_m8, tk_work))
                carry()
                link(nc.vector.match_replace(tk_work, tk_m8, tk_work, -1.0))
            loop(0, KSEL // 8, 2, best8)
            link(nc.vector.tensor_tensor(tk_mask, tk_work, tk_val, ALU.is_lt))
            link(nc.vector.tensor_tensor_scan(tk_pos, ones[0:E * B, :], tk_mask, 0.0, ALU.mult, ALU.add))
            nc.vector.tensor_tensor(tk_rank, tk_pos, tk_mask, ALU.mult).then_inc(s_tk, 1)

            def one_hot(n):
                rows = rvT[:, 0].rearrange("p k (e b) -> p k e b", e=E)
                link(nc.vector.tensor_copy(rk_s[:], rows[:, :, :, n]))
                for k in range(TB):
                    ins = nc.vector.tensor_tensor(sel[:, k].rearrange("p (e q) -> p e q", e=E),
                                                  rk_s[:, k].unsqueeze(2).broadcast_to([P, E, KSEL]),
                                                  iota1.unsqueeze(1).broadcast_to([P, E, KSEL]), ALU.is_equal)
                return ins

            dve.wait_ge(s_rv, 1)

            def gather(n):
                dve.wait_ge(s_gath, n)
                link(nc.vector.tensor_copy(mr_s[:, 0], mean1[:, n]))
                link(nc.vector.tensor_copy(mr_s[:, 1], rstd1[:, n]))
                normalised(n, mr_s[:, 0].unsqueeze(2), mr_s[:, 1].unsqueeze(2))
                one_hot(n).then_inc(s_sel, 1)
                dve.wait_ge(s_gath, n + 1)
                nc.vector.tensor_copy(csg[:, :, n, :], bank[1][:].rearrange("p (e q) -> p e q", e=E)).then_inc(s_gcs, 1)
            loop(0, B, 3, gather)
            dve.wait_ge(s_gcs, B)

            def expert(ep):
                for par in range(2):
                    n = ep * 2 + par
                    cg = csg[0:64, n].rearrange("p b q -> p (b q)")
                    sg = csg[64:128, n].rearrange("p b q -> p (b q)")
                    dve.wait_ge(s_q3, n + 1)
                    dve.wait_ge(s_sc, n)
                    nc.vector.tensor_tensor(t2q[0:64], bank[2][0:64], sg, ALU.mult)
                    nc.vector.tensor_tensor(t2k[0:64], bank[2][64:128], sg, ALU.mult)
                    nc.vector.tensor_tensor(qf[0:64], bank[0][0:64], cg, ALU.mult)
                    link(nc.vector.tensor_tensor(kf[0:64], bank[1][0:64], cg, ALU.mult))
                    nc.vector.tensor_tensor(qf[0:64], qf[0:64], t2q[0:64], ALU.add)
                    nc.vector.tensor_tensor(kf[0:64], kf[0:64], t2k[0:64], ALU.add).then_inc(s_rope, 1)
                    dve.wait_ge(s_sc, n + 1)
                    dve.wait_ge(s_pt, n)
                    link(nc.vector.scalar_tensor_tensor(s1[:], bank[4][:].rearrange("p (a m) -> p a m", a=TB), float(P) ** -0.5,
                                                        causal.unsqueeze(1).broadcast_to([P, TB, P]), ALU.mult, ALU.add))
                    link(nc.vector.tensor_reduce(rmax[:], s1[:], AX.X, ALU.max))
                    nc.vector.tensor_tensor(s1[:], s1[:], rmax.unsqueeze(2).broadcast_to([P, TB, P]), ALU.subtract).then_inc(s_sm, 1)
                    dve.wait_ge(s_pexp, n + 1)
                    link(nc.vector.tensor_reduce(rsum[:], s1[:], AX.X, ALU.add))
                    link(nc.vector.reciprocal(rinv[:], rsum[:]))
                    dve.wait_ge(s_yd, n + 1)
                    dve.wait_ge(s_ymv[par], ep * 32)
                    nc.vector.tensor_tensor(y_s[:, par], bank[7][:].rearrange("p (a m) -> p a m", a=TB),
                                            rinv.unsqueeze(2).broadcast_to([P, TB, P]), ALU.mult).then_inc(s_ys, 1)
            loop(0, E // 2, 10, expert)

            def scatter(n):
                dve.wait_ge(s_selTc, n)
                vals = rvT[:, 1].rearrange("p k (e b) -> p k e b", e=E)
                nc.vector.tensor_copy(vl_s[:], vals[:, :, :, n])
                link(one_hot(n))
                for k in range(TB):
                    ins = nc.vector.tensor_tensor(sel_w[:, k].rearrange("p (e q) -> p e q", e=E),
                                                  sel[:, k].rearrange("p (e q) -> p e q", e=E),
                                                  vl_s[:, k].unsqueeze(2).broadcast_to([P, E, KSEL]), ALU.mult)
                ins.then_inc(s_selw, 1)
                dve.wait_ge(s_scat, n + 1)
                nc.vector.tensor_tensor(x_all[:, n], bank[4][:].rearrange("p (k d) -> p k d", k=TB), x_all[:, n],
                                        ALU.add).then_inc(s_ffn, 1)
            dve.wait_ge(s_ymv[0], 32 * (E // 2))
            dve.wait_ge(s_ymv[1], 32 * (E // 2))
            loop(0, B, 2, scatter)

            dve.wait_ge(s_ffn, B)
            nc.vector.memset(bs6[64:128], 1.0).then_inc(s_bs6, 1)

            def split(raw, stk, par):
                nc.vector.tensor_copy(stk[0:64, par, 0], raw[0:64])
                link(nc.vector.tensor_copy(stk[64:128, par, 1], raw[64:128]))
                nc.vector.tensor_tensor(stk[64:128, par, 0], raw[0:64], stk[0:64, par, 0], ALU.subtract)
                return nc.vector.tensor_tensor(stk[0:64, par, 1], raw[64:128], stk[64:128, par, 1], ALU.subtract)

            def prep_u(g, q, par):
                dve.wait_ge(s_prep_free, prep_index(g, 1) + 1)
                if q is not None:
                    dve.wait_ge(s_f, (q - 1) * 16)
                split(u_raw, u_stk, par).then_inc(s_us, 1)

            def prep_v(g, par):
                dve.wait_ge(s_prep_free, prep_index(g, 2) + 1)
                link(split(v_raw, v_stk, par))
                nc.vector.tensor_copy(v_swp[0:64, par], v_stk[64:128, par])
                nc.vector.tensor_copy(v_swp[64:128, par], v_stk[0:64, par]).then_inc(s_vs_rdy, 1)

            def add_g(i, j):
                g = i * 8 + j
                dve.wait_ge(s_prep_full, prep_index(g, 0) + 1)
                nb = i if j else i - 1
                nc.vector.scalar_tensor_tensor(x_all[:, nb], prep_bank[:].rearrange("p (k d) -> p k d", k=TB),
                                               0.5 * FACTOR_SCALE ** 2, x_all[:, nb], ALU.mult, ALU.add).then_inc(s_prep_free, 1)

            def evac_o(g, j, o, k):
                dve.wait_ge(s_out, g * 8 + 4 * (o + 1))
                if k is not None:
                    dve.wait_ge(s_prep_full, k)
                nc.vector.tensor_scalar(o_s[j % 2][:, o], o_bank[o][:], sums[:, o, j % 2:j % 2 + 1], None, ALU.add)\
                  .then_inc(s_oe, 1)

            def split2(src, stk):
                link(nc.vector.tensor_copy(stk[:], src[:]))
                nc.vector.tensor_tensor(stk[64:128], src[64:128], stk[64:128], ALU.subtract).then_inc(s_stk, 1)

            def l1(step, L):
                kind, f = step
                s = L * NL + STEP_AT[step]
                if kind == "norm":
                    statistics(L, s_stats2)
                    dve.wait_ge(s_rstd2, L + 1)
                    normalised(L, mv_s[:, :, 0:1], rstd_s[:].unsqueeze(2)).then_inc(s_xn2, 1)
                elif kind in "kq" and kind != "":
                    nth = L * 2 + (1 if kind == "k" else 2)
                    dve.wait_ge(s_lf, s + 1)
                    nc.vector.tensor_scalar(kmin[:], l1_bank[:], 0.0, None, ALU.min).then_inc(s_min, 1)
                    dve.wait_ge(s_exp, nth)
                    nc.vector.scalar_tensor_tensor(kf32[:], l1_bank[:], 0.0, kexp[:], ALU.max, ALU.add).then_inc(s_le, 1)
                    dve.wait_ge(s_le, s + 1)
                    split2(kf32, k_stk if kind == "k" else q_stk)
                elif kind == "v":
                    dve.wait_ge(s_le, s + 1)
                    split2(kf32, vl_stk)
                elif kind == "A":
                    dve.wait_ge(s_lf, s + 1)
                    nc.vector.tensor_tensor(ab[:], l1_bank[:], (bs6 if f == NF - 1 else bs)[:], ALU.mult).then_inc(s_le, 1)
                    dve.wait_ge(s_le, s + 1)
                    link(nc.vector.tensor_tensor_scan(pre[:], ones[:], ab[:], 0.0, ALU.mult, ALU.add))
                elif kind in "CD":
                    r, half = round_of(kind, f)
                    dve.wait_ge(s_lf, s + 1)
                    if kind == "C" and f != 1:
                        dve.wait_ge(s_y, L * ROUNDS + max(r - 1, 0))
                    nc.vector.tensor_tensor(pc[half][:, r % 2], l1_bank[:], pre[:], ALU.mult).then_inc(s_le, 1)
                elif kind == "den":
                    dve.wait_ge(s_lf, s + 1)
                    nc.vector.tensor_scalar(small[:, 0:TB], l1_bank[:, 0:TB], 1e-6, None, ALU.max).then_inc(s_le, 1)
                    dve.wait_ge(s_le, s + 1)
                    link(nc.vector.reciprocal(small[:, TB:2 * TB], small[:, 0:TB]))
                    dve.wait_ge(s_yo, L + 1)
                    for k in range(TB):
                        ins = nc.vector.scalar_tensor_tensor(x_all[:, L, k], y_bank[:, k * P:(k + 1) * P], small[:, TB + k:TB + k + 1],
                                                             x_all[:, L, k], ALU.mult, ALU.add)
                    ins.then_inc(s_yfree, 1)
                elif kind == "gate":
                    dve.wait_ge(s_tanh, L * HC + f + 1)
                    nc.vector.scalar_tensor_tensor(gated[:], tg[:], 1.0, l1_bank[:], ALU.add, ALU.mult).then_inc(s_le, 1)
                elif kind == "up":
                    dve.wait_ge(s_lf, s + 1)
                    dve.wait_ge(s_le, s)
                    nc.vector.scalar_tensor_tensor(hid[:, f], gated[:], 0.5, l1_bank[:], ALU.mult, ALU.mult).then_inc(s_le, 1)
                elif kind == "down":
                    dve.wait_ge(s_lf, s + 1)
                    dve.wait_ge(s_yfree, L + 1)
                    nc.vector.tensor_tensor(x_all[:, L], l1_bank[:].rearrange("p (k d) -> p k d", k=TB), x_all[:, L],
                                            ALU.add).then_inc(s_le, 1)

            prep_u(-1, None, 0)
            prep_v(-1, 0)

            def iteration(i, attn, second):
                steps = iter(L1_STEPS if second else [])
                if not attn:
                    add_g(i, 0)
                    dve.wait_ge(s_prep_free, prep_index(i * 8, 0) + 1)
                    for st in steps:
                        l1(st, i - 1)
                    return
                for j in range(PAIRS):
                    g = i * 8 + j
                    for u in range(UNITS):
                        if u == 1 and (second or j):
                            add_g(i, j)
                        if u == 2:
                            prep_u(g, g + 1 if second or j else None, (j + 1) % 2)
                        if u == 3:
                            prep_v(g, (j + 1) % 2)
                        if u % TB == TB - 1:
                            evac_o(g, j, u // TB, prep_index(g - 1, 0) + 1 if second or j >= 2 else None)
                        if j * UNITS + u >= L1_FIRST_SLOT:
                            if j == 0 and u == L1_FIRST_SLOT and second:
                                dve.wait_ge(s_prep_free, prep_index(g, 0) + 1)
                            for st in [s for s in [next(steps, None)] if s]:
                                l1(st, i - 1)
                for st in steps:
                    l1(st, i - 1)

            iteration(0, True, False)
            links = [0]

            def body(i):
                iteration(i, True, True)
            loop(1, B, 3 * PAIRS + 2 + 3 + NF + 1, body)
            iteration(B, False, True)

        @block.scalar
        def _(act):
            def copy(dst, src):
                return nc.scalar.activation(dst, src, ACT.Copy)

            with act.Fori(0, B) as n:
                act.wait_ge(s_xT, n + 1)
                copy(xn1T[:, n], bank[0][:]).then_inc(s_xnT, 1)
                act.wait_ge(s_lg, n + 1)
                copy(lg8[0:E, n], bank[1][0:E]).then_inc(s_lgc, 1)
            act.wait_ge(s_lgd, 16)
            nc.scalar.activation(tk_work, lg[0:E * B], ACT.Exp, scale=-1.0).then_inc(s_ex, 1)
            act.wait_ge(s_tkT, 1)
            copy(rvT[:].rearrange("p a k c -> p (a k c)"), bank[2][:]).then_inc(s_rv, 1)
            with act.Fori(0, B) as n:
                act.wait_ge(s_gath, n + 1)
                copy(xgT[:, :, n, :], bank[0][:].rearrange("p (e q) -> p e q", e=E)).then_inc(s_gx, 1)

            with act.Fori(0, E // 2) as ep:
                for par in range(2):
                    n = ep * 2 + par
                    act.wait_ge(s_gx, B)
                    act.wait_ge(s_vd, n)
                    copy(xg_s[:], xgT[:, n].rearrange("p b q -> p (b q)")).then_inc(s_xgs, 1)
                    act.wait_ge(s_q3, n + 1)
                    act.wait_ge(s_sc, n)
                    copy(qf[64:128], bank[0][64:128])
                    copy(kf[64:128], bank[1][64:128]).then_inc(s_qk_hi, 1)
                    act.wait_ge(s_vd, n + 1)
                    act.wait_ge(s_av, n)
                    copy(v_s[:].rearrange("p a m -> p (a m)"), bank[3][:]).then_inc(s_vs, 1)
                    act.wait_ge(s_sm, n + 1)
                    nc.scalar.activation(s1[:], s1[:], ACT.Exp).then_inc(s_pexp, 1)
                    act.wait_ge(s_pt, n + 1)
                    copy(ptT[:].rearrange("p a m -> p (a m)"), bank[5][:]).then_inc(s_ptc, 1)
                    act.wait_ge(s_av, n + 1)
                    copy(avT[:].rearrange("p a m -> p (a m)"), bank[6][:]).then_inc(s_avc, 1)

            with act.Fori(0, B) as n:
                for e2 in range(E // 2):
                    act.wait_ge(s_selT, n * 4 + e2 + 1)
                    act.wait_ge(s_scat, n)
                    ins = copy(selT[:, e2], bank[e2][:])
                ins.then_inc(s_selTc, 1)

            act.wait_ge(s_ffn, B)

            def prep_raw(g, k, raw, total, par, q):
                act.wait_ge(s_prep_full, prep_index(g, k) + 1)
                if not (isinstance(g, int) and g < 0):
                    act.wait_ge(s_us if k == 1 else s_vs_rdy, g + 1)
                    act.wait_ge(s_prep_full, 4 if isinstance(g, int) and g == 0 else prep_index(g, 0))
                if q is not None:
                    act.wait_ge(s_oe, (q - 1) * 2)
                nc.scalar.activation(raw[:], prep_bank[:], ACT.Copy, accum_out=total[:, par:par + 1]).then_inc(s_prep_free, 1)

            def prep_tok(g, k, tok, par, q):
                act.wait_ge(s_prep_full, prep_index(g, k) + 1)
                if q is not None:
                    act.wait_ge(s_out, (q - 1) * 8)
                copy(tok[:, par].rearrange("p k c -> p (k c)"), prep_bank[:]).then_inc(s_prep_free, 1)

            def tanh_unit(i, n0):
                for n in (n0, n0 + 1):
                    act.wait_ge(s_f, i * 128 + n + 1)
                    if n0 >= 4:
                        act.wait_ge(s_out, i * 64 + n0 // 2 - 1)
                    elif not isinstance(i, int):
                        act.wait_ge(s_out, i * 64 + n0 // 2 - 1)
                    nc.scalar.activation(th[:, n % TH_SLOTS], f_bank[n % F_BANKS][:], ACT.Tanh,
                                         scale=0.5 * FACTOR_SCALE ** 2).then_inc(s_th, 1)

            def l1(step, L):
                kind, f = step
                s = L * NL + STEP_AT[step]
                if kind == "norm":
                    act.wait_ge(s_lf, s + 1)
                    copy(xn2T[:], l1_bank[:]).then_inc(s_le, 1)
                elif kind in "kq" and kind != "":
                    nth = L * 2 + (1 if kind == "k" else 2)
                    act.wait_ge(s_min, nth)
                    nc.scalar.activation(kexp[:], kmin[:], ACT.Exp).then_inc(s_exp, 1)
                elif kind == "v":
                    act.wait_ge(s_lf, s + 1)
                    act.wait_ge(s_stk, L * 3 + 2)
                    copy(kf32[:], l1_bank[:]).then_inc(s_le, 1)
                elif kind == "B":
                    act.wait_ge(s_lf, s + 1)
                    if f == NF - 1:
                        copy(bs6[0:64], l1_bank[0:64]).then_inc(s_le, 1)
                    else:
                        copy(bs[:], l1_bank[:]).then_inc(s_le, 1)
                elif kind == "den":
                    act.wait_ge(s_y, L * ROUNDS + ROUNDS)
                    copy(y_sb[:], y_bank[:]).then_inc(s_ysb, 1)
                elif kind == "gate":
                    act.wait_ge(s_lf, s + 1)
                    act.wait_ge(s_le, s)
                    nc.scalar.activation(tg[:], l1_bank[:], ACT.Tanh, scale=0.5).then_inc(s_tanh, 1)

            prep_raw(-1, 1, u_raw, sums[:, 1], 0, None)
            prep_raw(-1, 2, v_raw, sums[:, 0], 0, None)
            prep_tok(-1, 3, u_tok, 0, None)
            prep_tok(-1, 4, v_tok, 0, None)

            def iteration(i, attn, second):
                steps = iter(L1_STEPS if second else [])
                if attn:
                    tanh_unit(i, 0)
                    for j in range(PAIRS):
                        g = i * 8 + j
                        q = g + 1
                        for u in range(UNITS):
                            if j * UNITS + u < PAIRS * UNITS - 1:
                                tanh_unit(i, 2 * (j * UNITS + u + 1))
                            q1 = q if second or j else None
                            if u == 2:
                                prep_raw(g, 1, u_raw, sums[:, 1], (j + 1) % 2, q1)
                            if u == 3:
                                prep_raw(g, 2, v_raw, sums[:, 0], (j + 1) % 2, q1)
                            if u == 5:
                                prep_tok(g, 3, u_tok, (j + 1) % 2, q1)
                            if u == 6:
                                prep_tok(g, 4, v_tok, (j + 1) % 2, q1)
                            if j * UNITS + u >= L1_FIRST_SLOT:
                                for st in [s for s in [next(steps, None)] if s]:
                                    l1(st, i - 1)
                for st in steps:
                    l1(st, i - 1)

            iteration(0, True, False)
            with act.Fori(1, B) as i:
                iteration(i, True, True)
            iteration(B, False, True)

        @block.tensor
        def _(pe):
            def mm(out, lhsT, rhs, start=True, stop=True):
                return nc.tensor.matmul(out, lhsT, rhs, start=start, stop=stop)

            pe.wait_ge(s_const, 16 * (len(consts) + len(phase_consts)))
            with pe.Fori(0, B) as n:
                pe.wait_ge(s_xn, n + 1)
                pe.wait_ge(s_xnT, n)
                for k in range(TB):
                    ins = nc.tensor.transpose(bank[0][:, k * P:(k + 1) * P], xn_s[:, k], ident[:])
                ins.then_inc(s_xT, 1)
                pe.wait_ge(s_xnT, n + 1)
                pe.wait_ge(s_lgc, n)
                mm(bank[1][0:E], wr_w[:], xn1T[:, n]).then_inc(s_lg, 1)
            pe.wait_ge(s_tk, 1)
            for a, src in enumerate((tk_rank, tk_val)):
                for k in range(TB):
                    ins = nc.tensor.transpose(bank[2][:, (a * TB + k) * 64:(a * TB + k + 1) * 64], src[:, k * P:(k + 1) * P],
                                              ident[0:64, 0:64])
            ins.then_inc(s_tkT, 1)
            with pe.Fori(0, B) as n:
                pe.wait_ge(s_sel, n + 1)
                pe.wait_ge(s_gx, n)
                pe.wait_ge(s_gcs, n)
                for k in range(TB):
                    mm(bank[0][:], xn_s[:, k], sel[:, k], k == 0, k == TB - 1)
                for k in range(TB):
                    ins = mm(bank[1][:], table[:, k], sel[:, k], k == 0, k == TB - 1)
                ins.then_inc(s_gath, 1)
            pe.wait_ge(s_gx, B)
            pe.wait_ge(s_gcs, B)
            with pe.Fori(0, E // 2) as ep:
                for par in range(2):
                    n = ep * 2 + par
                    w = we[:, par]
                    xg = xgT[:, n].rearrange("p b q -> p (b q)")
                    pe.wait_ge(s_we[par], ep * 16 + 16)
                    pe.wait_ge(s_rope, n)
                    pe.wait_ge(s_qk_hi, n)
                    mm(bank[0][:], w[:, 0:P], xg)
                    mm(bank[1][:], w[:, P:2 * P], xg)
                    mm(bank[2][:], w[:, 2 * P:3 * P], xg).then_inc(s_q3, 1)
                    pe.wait_ge(s_vs, n)
                    pe.wait_ge(s_xgs, n + 1)
                    for a in range(TB):
                        ins = mm(bank[3][:, a * P:(a + 1) * P], xg_s[:, a * P:(a + 1) * P], w[:, 3 * P:4 * P])
                    ins.then_inc(s_vd, 1)
                    pe.wait_ge(s_rope, n + 1)
                    pe.wait_ge(s_qk_hi, n + 1)
                    pe.wait_ge(s_sm, n)
                    for a in range(TB):
                        ins = mm(bank[4][:, a * P:(a + 1) * P], qf[:, a * P:(a + 1) * P], kf[:, a * P:(a + 1) * P])
                    ins.then_inc(s_sc, 1)
                    pe.wait_ge(s_pexp, n + 1)
                    pe.wait_ge(s_ptc, n)
                    for a in range(TB):
                        ins = nc.tensor.transpose(bank[5][:, a * P:(a + 1) * P], s1[:, a], ident[:])
                    ins.then_inc(s_pt, 1)
                    pe.wait_ge(s_ptc, n + 1)
                    pe.wait_ge(s_vs, n + 1)
                    pe.wait_ge(s_avc, n)
                    for a in range(TB):
                        ins = mm(bank[6][:, a * P:(a + 1) * P], v_s[:, a], ptT[:, a])
                    ins.then_inc(s_av, 1)
                    pe.wait_ge(s_avc, n + 1)
                    pe.wait_ge(s_ys, n)
                    for a in range(TB):
                        ins = mm(bank[7][:, a * P:(a + 1) * P], avT[:, a], w[:, 4 * P:5 * P])
                    ins.then_inc(s_yd, 1)
            pe.wait_ge(s_ymv[0], 16 * E)
            pe.wait_ge(s_ymv[1], 16 * E)
            with pe.Fori(0, B) as n:
                pe.wait_ge(s_selw, n + 1)
                pe.wait_ge(s_selTc, n)
                for e2 in range(E // 2):
                    for k in range(TB):
                        ins = nc.tensor.transpose(bank[e2][:, k * P:(k + 1) * P], sel_w[:, k, e2 * P:(e2 + 1) * P], ident[:])
                    ins.then_inc(s_selT, 1)
                pe.wait_ge(s_selTc, n + 1)
                pe.wait_ge(s_ffn, n)
                for k in range(TB):
                    for e2 in range(E // 2):
                        ins = mm(bank[4][:, k * P:(k + 1) * P], selT[:, e2, k * P:(k + 1) * P], y_all[:, n, e2], e2 == 0, e2 == E // 2 - 1)
                ins.then_inc(s_scat, 1)

            pe.wait_ge(s_ffn, B)
            pe.wait_ge(s_prep_w, 1)
            pe.wait_ge(s_ones, 2)

            def prep(g, k, j, i_next):
                n = prep_index(g, k)
                pe.wait_ge(s_prep_free, n)
                if k in (1, 2):
                    ins = mm(prep_bank[:], (uT_w if k == 1 else vT_w)[:, j * P:(j + 1) * P], xn1T[:, i_next])
                else:
                    if k == 3:
                        pe.wait_ge(s_prep_free, prep_index(g, 2) + 1)
                    for t in range(TB):
                        ins = nc.tensor.transpose(prep_bank[:, t * P:(t + 1) * P], (u_raw if k == 3 else v_raw)[:, t * P:(t + 1) * P],
                                                  ident[:])
                ins.then_inc(s_prep_full, 1)

            def project(g, j):
                pe.wait_ge(s_prep_free, prep_index(g, 0))
                pe.wait_ge(s_oe, g * 2)
                was = (j - 1) % PAIRS
                for t in range(TB):
                    for o, w in enumerate((u_w, v_w)):
                        ins = mm(prep_bank[:, t * P:(t + 1) * P], o_s[was % 2][:, o, t * P:(t + 1) * P], w[:, was], o == 0, o == 1)
                ins.then_inc(s_prep_full, 1)

            def scores(i, un):
                j, u = un // UNITS, un % UNITS
                par, o, blk = j % 2, u // TB, u % TB
                if u == 0:
                    pe.wait_ge(s_us, i * PAIRS + j + 1)
                    pe.wait_ge(s_vs_rdy, i * PAIRS + j + 1)
                for h in range(2):
                    n = 2 * un + h
                    if n >= F_BANKS:
                        pe.wait_ge(s_th, i * 128 + n - F_BANKS + 1)
                    elif not isinstance(i, int):
                        pe.wait_ge(s_th, i * 128 - (1, 0, 2)[n])
                    bk = f_bank[n % F_BANKS]
                    cols = slice(blk * P, (blk + 1) * P)
                    if o == 0:
                        mm(bk[:], v_stk[:, par, h, cols], u_stk[:, par, h], True, False)
                        ins = mm(bk[:], v_swp[:, par, h, cols], u_stk[:, par, h], False, True)
                    else:
                        mm(bk[:], u_stk[:, par, h, cols], v_stk[:, par, h], True, False)
                        ins = mm(bk[:], u_stk[:, par, h, cols], v_swp[:, par, h], False, True)
                    ins.then_inc(s_f, 1)

            def weighted(i, un, first_batch):
                j, u = un // UNITS, un % UNITS
                par, o, blk = j % 2, u // TB, u % TB
                g = i * PAIRS + j
                if u == 0:
                    pe.wait_ge(s_prep_free, 4 if first_batch and j == 0 else prep_index(g - 1, 4) + 1)
                if blk == 0 and not (first_batch and j == 0):
                    pe.wait_ge(s_oe, g * 2 - 1 + o)
                pe.wait_ge(s_th, i * 128 + 2 * un + 2)
                tok = (v_tok, u_tok)[o]
                for h in range(2):
                    rows = slice(64 * h, 64 * h + 64)
                    ins = mm(o_bank[o][rows], tok[:, par, blk, rows], th[:, (2 * un + h) % TH_SLOTS], blk == 0, blk == TB - 1)
                ins.then_inc(s_out, 1)

            def spread(step, f):
                at0 = E_AT[step] + f * P
                src = {"A": k_stk, "B": vl_stk, "C": q_stk, "D": q_stk}[step]
                ins = mm(l1_bank[:], e_str[:, at0:at0 + P], src[:], True, f < 2)
                if f >= 2:
                    ins = mm(l1_bank[:], e_swp[:, at0:at0 + P], src[:], False, True)
                return ins

            def y_round(r, L):
                pe.wait_ge(s_le, L * NL + STEP_AT[("C", 1) if r == 0 else ("D", r + 1)] + 1)
                if r == 0:
                    pe.wait_ge(s_yfree, L)
                mm(y_bank[0:64], top_w[:, r], pc[0][:, r % 2], r == 0, r == ROUNDS - 1)
                mm(y_bank[64:128], bot_w[:, r], pc[1][:, r % 2], r == 0, r == ROUNDS - 1).then_inc(s_y, 1)

            def l1(step, L):
                kind, f = step
                s = L * NL + STEP_AT[step]
                if kind == "A" and f >= 2:
                    y_round(f - 2, L)
                if kind == "den":
                    y_round(ROUNDS - 1, L)
                if kind == "norm":
                    pe.wait_ge(s_xn2, L + 1)
                if kind == "B" and f == 0:
                    pe.wait_ge(s_stk, L * 3 + 3)
                pe.wait_ge(s_le, s)
                if kind == "norm":
                    for t in range(TB):
                        ins = nc.tensor.transpose(l1_bank[:, t * P:(t + 1) * P], xn_s[:, t], ident[:])
                elif kind in ("k", "q", "v"):
                    ins = mm(l1_bank[:], {"k": kk_w, "q": qq_w, "v": vv_w}[kind][:], xn2T[:])
                elif kind in ("A", "B", "C", "D"):
                    ins = spread(kind, f)
                elif kind == "den":
                    for t in range(TB):
                        ins = mm(l1_bank[:, t:t + 1], pc[0][:, (ROUNDS - 1) % 2, t * P:(t + 1) * P], zsel[:])
                elif kind in ("gate", "up"):
                    ins = mm(l1_bank[:], (wg if kind == "gate" else wu)[:, f * P:(f + 1) * P], xn2T[:])
                elif kind == "down":
                    for t in range(TB):
                        for h in range(HC):
                            ins = mm(l1_bank[:, t * P:(t + 1) * P], hid[:, h, t * P:(t + 1) * P], wd[:, h], h == 0, h == HC - 1)
                ins.then_inc(s_lf, 1)
                if kind == "den":
                    pe.wait_ge(s_ysb, L + 1)
                    for t in range(TB):
                        ins = mm(y_bank[:, t * P:(t + 1) * P], y_sb[:, t * P:(t + 1) * P], wo2[:])
                    ins.then_inc(s_yo, 1)

            for k in range(1, 5):
                prep(-1, k, 0, 0)

            def iteration(i, attn, second):
                steps = iter(L1_STEPS if second else [])
                if not attn:
                    project(i * PAIRS, 0)
                    for st in steps:
                        l1(st, i - 1)
                    return
                scores(i, 0)
                for j in range(PAIRS):
                    g = i * PAIRS + j
                    for u in range(UNITS):
                        un = j * UNITS + u
                        if un < PAIRS * UNITS - 1:
                            scores(i, un + 1)
                        weighted(i, un, not second)
                        if u == 1 and (second or j):
                            project(g, j)
                        if u in (2, 3, 5, 6):
                            prep(g, {2: 1, 3: 2, 5: 3, 6: 4}[u], (j + 1) % PAIRS, i if j < PAIRS - 1 else i + 1)
                        if un >= L1_FIRST_SLOT:
                            for st in [x for x in [next(steps, None)] if x]:
                                l1(st, i - 1)
                for st in steps:
                    l1(st, i - 1)

            iteration(0, True, False)
            with pe.Fori(1, B) as i:
                iteration(i, True, True)
            iteration(B, False, True)


def tables():
    half = NROT // 2
    inv = (np.float32(1.0) / np.float32(10000.0) ** (np.arange(half, dtype=np.float32) * np.float32(2.0) / np.float32(NROT))).astype(np.float32)
    ang = np.arange(T, dtype=np.float32)[:, None] * inv
    cos, sin = np.cos(ang).astype(np.float32), np.sin(ang).astype(np.float32)
    at = np.arange(P)
    same = at[:, None] // KSEL == at[None, :] // KSEL
    seen = same & (at[:, None] >= at[None, :])
    return {
        "table": np.concatenate([cos, cos, -sin, sin], axis=1),
        "causal": np.where(seen, 0.0, MASKED).astype(np.float32),
        "ident": np.eye(P, dtype=np.float32),
        "iota1": np.tile(np.arange(1, KSEL + 1, dtype=np.float32), (P, 1)),
        "zsel": (at >= 64).astype(np.float32)[:, None],
    }


def laid_out(x):
    f32 = np.float32
    wqkv, wo = x["L0_ffn_Wqkv"], x["L0_ffn_Wo"]
    turned = np.concatenate([np.arange(32, 64), np.arange(32)])
    wq, wk, wv = wqkv[:, :, 0:P], wqkv[:, :, P:2 * P], wqkv[:, :, 2 * P:]
    we = np.concatenate([wq, wk, wq[:, :, turned], wk[:, :, turned], wv, wo], axis=2)

    eye = np.eye(DH, dtype=f32)
    ea, eb, ed = (np.zeros((DH, NF * P), f32) for _ in range(3))
    top, bot = (np.zeros((NF * P, DH), f32) for _ in range(2))
    f = 0
    for n in range(DH // LEAF):
        for i in range(LEAF):
            for j in range(LEAF):
                ea[:, f], eb[:, f] = eye[:, n * LEAF + i], eye[:, n * LEAF + j]
                top[f] = eye[n * LEAF + i]
                f += 1
    for lv, (bs, r, nodes) in enumerate(LEVELS):
        UL, VR, UR, VL = (x[f"L1_attn_{w}{lv}"] for w in ("UL", "VR", "UR", "VL"))
        for n in range(nodes):
            left = slice(2 * bs * n, 2 * bs * n + bs)
            right = slice(2 * bs * n + bs, 2 * bs * (n + 1))
            for i in range(r):
                for j in range(r):
                    ea[left, f], eb[right, f], ed[left, f] = UL[:, i], VR[:, j], VL[:, i]
                    top[f, left], bot[f, right] = UL[:, i], UR[:, j]
                    f += 1
    ea[:, f:f + DH] = eb[:, f:f + DH] = eye
    assert f + DH == NF * P
    e = np.concatenate([ea, eb, ed[:, 2 * P:]], axis=1)
    tiles = lambda a: a.reshape(NF, P, DH)
    top_w = np.stack([tiles(top)[t] for t in (0, 2, 3, 4, 5, 6)], axis=1)
    bot_w = np.stack([tiles(top)[1]] + [tiles(bot)[t] for t in (2, 3, 4, 5, 6)], axis=1)
    twice = lambda w: np.concatenate([w, w], axis=1)
    wd = x["L1_ffn_w_down"].T.reshape(HC, P, D).transpose(1, 0, 2).reshape(P, HIDDEN)
    return {
        "x": x["L0_attn_qz"],
        "u": x["L0_attn_ternary_factor_u"], "v": x["L0_attn_ternary_factor_v"],
        "uT": x["L0_attn_ternary_factor_u"].T, "vT": x["L0_attn_ternary_factor_v"].T,
        "wrT": x["L0_ffn_Wr"].T, "we": we,
        "wk2": twice(x["L1_attn_Wk"]), "wq2": twice(x["L1_attn_Wq"]), "wv2": twice(x["L1_attn_Wv"]),
        "wo2": np.concatenate([x["L1_attn_Wo"]] * 2, axis=0),
        "top": top_w, "bot": bot_w, "e": np.concatenate([e, e], axis=0),
        "wi": np.stack([x["L1_ffn_w_gate"].T, x["L1_ffn_w_up"].T, wd], axis=1),
    }


def kernel(**inputs):
    import concourse.bacc as bacc
    from concourse.bass_utils import run_bass_kernel_spmd

    nc = bacc.Bacc("TRN2", target_bir_lowering=False, num_devices=1)
    arrays, io = {}, {}
    for name, a in {**laid_out({k: np.asarray(v) for k, v in inputs.items()}), **tables()}.items():
        a = np.ascontiguousarray(a)
        arrays[f"in_{name}"] = a
        io[name] = nc.dram_tensor(f"in_{name}", a.shape, mybir.dt.from_np(a.dtype), kind="ExternalInput").ap()
    io["out"] = nc.dram_tensor("out_0", (B, T, D), F32, kind="ExternalOutput").ap()
    build(nc, io)
    return run_bass_kernel_spmd(nc, [arrays], core_ids=[0]).results[0]["out_0"]
```

```python
from contextlib import ExitStack

import concourse.bass as bass
import numpy as np
from concourse import mybir

F32 = mybir.dt.float32
F32R = mybir.dt.float32r
I32 = mybir.dt.int32
ALU = mybir.AluOpType
ACT = mybir.ActivationFunctionType
AX = mybir.AxisListType

P = 128
B, T, D = 8, 512, 128
TB = T // P
EPS = 1e-5

C, R = 16, 64
PAIRS = C // 2
FACTOR_SCALE = 0.03125

E, KSEL = 8, 64
NROT = 64
EW = 3 * P + 2 * NROT + P
MASKED = -3.0e38
NPICK = 2 + 2 * E

DH, LEAF = 64, 4
LEVELS = [(4, 4, 8), (8, 8, 4), (16, 8, 2), (32, 8, 1)]
NF = 7
ROUNDS = 6
HIDDEN = 384
HC = HIDDEN // P
W_SCALE = 1.0 / 127.0

UNITS = 2 * TB
F_BANKS = 3
TH_SLOTS = 4

L1_STEPS = [("norm", 0), ("k", 0), ("q", 0), ("v", 0)]
for _f in range(NF):
    L1_STEPS += [("B", _f), ("A", _f), ("C", _f)] + ([("D", _f)] if _f >= 2 else [])
L1_STEPS += [("den", 0)]
for _h in range(HC):
    L1_STEPS += [("gate", _h), ("up", _h)]
L1_STEPS += [("down", 0)]
NL = len(L1_STEPS)
STEP_AT = {s: n for n, s in enumerate(L1_STEPS)}
L1_FIRST_SLOT = 3


def round_of(kind, f):
    if f < 2:
        return 0, f
    return f - 1, 0 if kind == "C" else 1


def prep_index(g, k):
    return k - 1 if isinstance(g, int) and g < 0 else g * 5 + 3 + k


def build(nc, io):
    ctx = ExitStack()
    with ctx:
        def sb(name, shape, dt=F32):
            return ctx.enter_context(nc.sbuf_tensor(name, shape, dt))

        def sem(name):
            return ctx.enter_context(nc.semaphore(name))

        bank = [ctx.enter_context(nc.psum_tensor(f"bank{n}", [P, 512], F32)) for n in range(8)]
        f_bank = bank[0:F_BANKS]
        o_bank = bank[3:5]
        prep_bank, l1_bank, y_bank = bank[5], bank[6], bank[7]

        x_all = sb("x_all", [P, B, TB, D])
        xn1T = sb("xn1T", [P, B + 1, T])
        ident = sb("ident", [P, P])
        ones = sb("ones", [P, 512])
        uT_w, vT_w = sb("uT_w", [P, C * R]), sb("vT_w", [P, C * R])
        u_w, v_w = sb("u_w", [P, PAIRS, D]), sb("v_w", [P, PAIRS, D])
        kk_w, qq_w, vv_w = sb("kk_w", [P, P]), sb("qq_w", [P, P]), sb("vv_w", [P, P])
        wo2 = sb("wo2", [P, D])
        top_w, bot_w = sb("top_w", [P, ROUNDS, DH]), sb("bot_w", [P, ROUNDS, DH])
        zsel = sb("zsel", [P, 1])
        wg, wu = sb("wg", [P, HIDDEN]), sb("wu", [P, HIDDEN])
        wd = sb("wd", [P, HC, D])
        NA, NB_, ND = NF * P, NF * P, (NF - 2) * P
        e_str = sb("e_str", [P, NA + NB_ + ND], F32R)
        e_swp = sb("e_swp", [P, NA + NB_ + ND], F32R)
        E_AT = {"A": 0, "B": NA, "C": NA, "D": NA + NB_ - 2 * P}
        u_stk, v_stk, v_swp = (sb(n, [P, 2, 2, T], F32R) for n in ("u_stk", "v_stk", "v_swp"))
        k_stk, q_stk, vl_stk = (sb(n, [P, T], F32R) for n in ("k_stk", "q_stk", "vl_stk"))
        stats = sb("stats", [P, TB, 6])
        mv_s, rstd_s, ve = sb("mv_s", [P, TB, 2]), sb("rstd_s", [P, TB]), sb("ve", [P, TB])
        mr_s = sb("mr_s", [P, 2, 2, TB])
        mv1, ve1, rstd1 = sb("mv1", [P, B, TB, 2]), sb("ve1", [P, B, TB]), sb("rstd1", [P, B, TB])
        powc = sb("powc", [P, 1])
        sel_r = sb("sel_r", [P, TB, E * KSEL], F32R)
        idle = sb("idle", [P, 1])
        xn_s = sb("xn_s", [P, TB, D])
        sums = sb("sums", [P, 2, 2])
        small = sb("small", [P, 8])

        ARENA = 21800
        arena = sb("arena", [P, ARENA])
        at = [0]

        def take(*shape):
            n = int(np.prod(shape))
            a = arena[:, at[0]:at[0] + n]
            at[0] += n
            assert at[0] <= ARENA, at[0]
            if len(shape) == 2:
                return a.rearrange("p (a b) -> p a b", a=shape[0])
            if len(shape) == 3:
                return a.rearrange("p (a b c) -> p a b c", a=shape[0], b=shape[1])
            return a

        xgT = take(E, B, KSEL)
        csg = take(E, B, KSEL)
        y_all = take(B, E // 2, D)
        rvT = take(2, TB, E * B)
        rk_s = take(2, TB, E)
        iota1 = take(KSEL)
        tokens = take(T)
        picks = take(B, (E // 2) * NPICK)
        iv_s = take(2, 2, E // 2)
        token_at = take(TB)
        causal = take(P)
        we, wo_e = take(2, EW - P), take(2, P)
        mark_experts = at[0]
        xg_s = take(T)
        t2q, t2k = take(T), take(T)
        qf, kf = take(T), take(T)
        v_s, s1, ptT, avT = take(TB, P), take(TB, P), take(TB, P), take(TB, P)
        y_s = take(2, TB, P)
        nmax, rsum, rinv = take(TB), take(TB), take(TB)
        at[0] = mark_experts
        wr_w = take(E)
        lg8 = take(B, T)
        lg = take(T)
        xn_g = take(2, TB, D)
        assert at[0] <= ARENA
        table = take(TB, P)
        at[0] = 0
        selT = take(2, E // 2, T)
        sels = [sel_r, v_stk[:].rearrange("p a b t -> p (a b) t")]
        xn_hl = u_stk
        table_hl = v_swp[:, 0]
        values_hl = [v_swp[:, 1, par, 0:TB * NPICK].rearrange("p (k c) -> p k c", k=TB) for par in range(2)]
        tk_val, tk_work, tk_mask, tk_pos, tk_rank = (xgT[0:E * B, e].rearrange("p b k -> p (b k)") for e in range(5))
        tk_m8 = small[0:E * B, 0:8]
        at[0] = 0
        e_raw = take(NA + NB_ + ND)
        wi = take(3 * HIDDEN).bitcast(I32)
        at[0] = 0
        u_raw, v_raw = take(T), take(T)
        u_tok, v_tok = take(2, TB, P), take(2, TB, P)
        th = take(TH_SLOTS, T)
        o_s = [take(2, T), take(2, T)]
        xn2T, kmin, kexp, kf32, bs, bs6, ab, pre = (take(T) for _ in range(8))
        pc = [take(2, T), take(2, T)]
        y_sb, tg, gated = take(T), take(T), take(T)
        hid = take(HC, T)

        s_stage, s_const, s_x = sem("stage_loaded"), sem("consts_loaded"), [sem("x_half0_loaded"), sem("x_half1_loaded")]
        s_prep_w, s_ones, s_powc = sem("weights_split"), sem("ones_set"), sem("powc_set")
        s_stats, s_rstd = sem("stats_ready"), sem("rstd_ready")
        s_xn, s_xT, s_xnT = sem("xn_ready"), sem("xn_transposed"), sem("xn1T_ready")
        s_lg, s_lgc, s_lgd = sem("logits_done"), sem("logits_copied"), sem("logits_moved")
        s_ex, s_tk, s_tkT, s_rv = sem("router_exp"), sem("topk_done"), sem("topk_transposed"), sem("ranks_ready")
        s_sel, s_gath, s_gx = sem("sel_ready"), sem("gathered"), sem("gather_copied")
        s_we, s_wo = [sem("expert_w0"), sem("expert_w1")], [sem("expert_wo0"), sem("expert_wo1")]
        s_q3, s_rope, s_vd, s_vs = sem("qkr_done"), sem("rope_done"), sem("expert_v_done"), sem("expert_v_copied")
        s_sc, s_sm, s_pexp, s_pt, s_ptc = (sem(n) for n in ("scores_done", "shifted", "probs_ready", "probsT_done", "probsT_copied"))
        s_av, s_avc, s_yd, s_ys = (sem(n) for n in ("av_done", "av_copied", "expert_y_done", "expert_y_scaled"))
        s_ymv = [sem("expert_y_moved0"), sem("expert_y_moved1")]
        s_qk_hi, s_xgs = sem("qk_passed_rows"), sem("picked_copied")
        s_selw, s_scat, s_ffn = (sem(n) for n in ("selT_ready", "scattered", "ffn_added"))
        s_chain = sem("dve_chain")
        s_prep_full, s_prep_free = sem("prep_bank_full"), sem("prep_bank_free")
        s_us, s_vs_rdy = sem("u_stack_ready"), sem("v_stack_ready")
        s_f, s_th, s_out, s_oe = sem("scores_full"), sem("tanh_done"), sem("unit_done"), sem("o_evacuated")
        s_lf, s_le = sem("l1_bank_full"), sem("l1_bank_free")
        s_stats2, s_rstd2, s_xn2 = sem("l1_stats"), sem("l1_rstd"), sem("l1_xn")
        s_min, s_exp, s_stk, s_tanh = sem("l1_min"), sem("l1_exp"), sem("l1_stack"), sem("l1_tanh")
        s_y, s_ysb, s_yo, s_yfree = sem("l1_y"), sem("l1_y_copied"), sem("l1_y_out"), sem("l1_y_bank_free")
        s_st = sem("stored")

        consts = [(ident, io["ident"]), (uT_w, io["uT"]), (vT_w, io["vT"]),
                  (u_w, io["u"].rearrange("(j p) d -> p j d", p=P)), (v_w, io["v"].rearrange("(j p) d -> p j d", p=P)),
                  (kk_w, io["wk2"]), (qq_w, io["wq2"]), (vv_w, io["wv2"]), (wo2, io["wo2"]),
                  (top_w, io["top"]), (bot_w, io["bot"]), (zsel, io["zsel"])]
        phase_consts = [(wr_w, io["wrT"]), (table, io["table"].rearrange("(k p) c -> p k c", p=P)),
                        (causal, io["causal"]), (iota1, io["iota1"]),
                        (tokens, io["tokens"]), (token_at, io["token_at"])]
        wi_v = wi.rearrange("p (a b) -> p a b", a=3)

        def pairs(fori, body, tail=0):
            for n in range(2):
                body(n, n)
            fori(1, (B - tail) // 2, lambda m: [body(m * 2 + par, par) for par in range(2)])
            for n in range(B - tail, B):
                body(n, n % 2)

        def lagged(fori, first, second):
            def both(n, par):
                first(n + 1, 1 - par)
                second(n, par)
            first(0, 0)
            for n in range(2):
                both(n, n)
            fori(1, B // 2 - 1, lambda m: [both(m * 2 + par, par) for par in range(2)])
            both(B - 2, 0)
            second(B - 1, 1)

        def fori_of(engine):
            def fori(lo, hi, body):
                with engine.Fori(lo, hi) as m:
                    body(m)
            return fori

        def later(n):
            return not (isinstance(n, int) and n < 2)

        def after_first(n):
            return not (isinstance(n, int) and n < 1)

        block = ctx.enter_context(nc.Block())

        @block.sync
        def _(sp):
            half_b = B // 2
            for h in range(2):
                sp.dma_start(x_all[:, h * half_b:(h + 1) * half_b],
                             io["x"][h * half_b:(h + 1) * half_b].rearrange("b (k p) d -> p b k d", p=P)).then_inc(s_x[h], 16)
            for dst, src in consts + phase_consts:
                sp.dma_start(dst[:], src).then_inc(s_const, 16)
            for par in range(2):
                sp.dma_start(we[:, par], io["we"][par, :, 0:EW - P]).then_inc(s_we[par], 16)
                sp.dma_start(wo_e[:, par], io["we"][par, :, EW - P:EW]).then_inc(s_wo[par], 16)
            sp.wait_ge(s_lgc, B)
            sp.dma_start(lg[0:E * B].rearrange("q t -> q t"), lg8[0:E].rearrange("e b t -> e b t")).then_inc(s_lgd, 16)

            def load_qkv(n, par):
                sp.wait_ge(s_vd, n + 1)
                sp.dma_start(we[:, par], io["we"][n + 2, :, 0:EW - P]).then_inc(s_we[par], 16)

            def load_wo(n, par):
                sp.wait_ge(s_yd, n + 1)
                sp.dma_start(wo_e[:, par], io["we"][n + 2, :, EW - P:EW]).then_inc(s_wo[par], 16)

            def move_rows(n, ep, par):
                sp.wait_ge(s_ys, n + 1)
                for half in range(2):
                    sp.dma_start(y_all[64 * par:64 * par + 64].rearrange("p (q r) e d -> p q r e d", r=2)[:, :, half, ep, :],
                                 y_s[64 * half:64 * half + 64, par]).then_inc(s_ymv[par], 16)

            load_qkv(0, 0)
            load_qkv(1, 1)
            with sp.Fori(0, E // 2 - 2) as m:
                for par in range(2):
                    n = m * 2 + par
                    load_wo(n, par)
                    move_rows(n, m, par)
                    load_qkv(n + 2, par)
            for par in range(2):
                load_wo(E - 4 + par, par)
                move_rows(E - 4 + par, E // 2 - 2, par)
            for par in range(2):
                move_rows(E - 2 + par, E // 2 - 1, par)
            with sp.Fori(0, B) as n:
                sp.wait_ge(s_le, n * NL + NL)
                sp.dma_start(io["out"][n].rearrange("(k p) d -> p k d", p=P), x_all[:, n]).then_inc(s_st, 16)
            sp.wait_ge(s_st, 16 * B)

        @block.gpsimd
        def _(pool):
            pool.memset(powc[:], -0.5).then_inc(s_powc, 1)
            pool.memset(ones[:], 1.0).then_inc(s_ones, 1)
            pool.memset(xn1T[:, B, :], 0.0).then_inc(s_ones, 1)
            pool.dma_start(e_raw[:, 0:NA + NB_ + ND], io["e"]).then_inc(s_stage, 16)
            pool.dma_start(wi_v[:], io["wi"]).then_inc(s_stage, 16)
            pool.wait_ge(s_powc, 1)
            for h in range(2):
                half = slice(h * B // 2, (h + 1) * B // 2)
                pool.wait_ge(s_stats, h + 1)
                pool.tensor_tensor(rstd1[:, half], ve1[:, half], powc[:].unsqueeze(2).broadcast_to([P, B // 2, TB]), ALU.pow)\
                    .then_inc(s_rstd, 1)
            with pool.Fori(0, B) as n:
                pool.wait_ge(s_stats2, n + 1)
                pool.tensor_tensor(rstd_s[:], ve[:], powc[:].broadcast_to([P, TB]), ALU.pow).then_inc(s_rstd2, 1)

        @block.vector
        def _(dve):
            chain = [0, 0]

            def link(ins):
                ins.then_inc(s_chain, 1)
                chain[1] += 1
                dve.wait_ge(s_chain, chain[0] + chain[1])

            def carry():
                nc.vector.memset(idle[:], 0.0)

            def loop(lo, hi, links, body):
                first = chain[0] + chain[1]
                with dve.Fori(lo, hi) as n:
                    chain[0], chain[1] = (n - lo if lo else n) * links + first, 0
                    body(n)
                    assert chain[1] == links, chain
                chain[0], chain[1] = first + (hi - lo) * links, 0

            def variances(n, mv):
                carry()
                for k in range(TB):
                    ins = nc.vector.bn_stats(stats[:, k], x_all[:, n, k])
                link(ins)
                carry()
                for k in range(TB):
                    ins = nc.vector.bn_aggr(mv[:, k], stats[:, k])
                return ins

            def normalised(dst, n, mean, inv):
                for k in range(TB):
                    ins = nc.vector.tensor_scalar(dst[:, k], x_all[:, n, k], mean[:, k], inv[:, k],
                                                  ALU.subtract, ALU.mult)
                return ins

            def first_norm(n, par):
                nc.vector.tensor_copy(mr_s[:, par, 0], mv1[:, n, :, 0])
                link(nc.vector.tensor_copy(mr_s[:, par, 1], rstd1[:, n]))
                return normalised(xn_g[:, par], n, mr_s[:, par, 0].unsqueeze(2), mr_s[:, par, 1].unsqueeze(2))

            for h in range(2):
                half = slice(h * B // 2, (h + 1) * B // 2)
                dve.wait_ge(s_x[h], 16)

                def half_statistics(n):
                    link(variances(n, mv_s))
                    link(nc.vector.tensor_copy(mv1[:, n], mv_s[:]))
                loop(h * B // 2, (h + 1) * B // 2, 3, half_statistics)
                nc.vector.tensor_scalar(ve1[:, half], mv1[:, half, :, 1], EPS, None, ALU.add).then_inc(s_stats, 1)

            dve.wait_ge(s_stage, 32)
            dve.wait_ge(s_const, 16 * (len(consts) + len(phase_consts)))
            nc.vector.tensor_copy(table_hl[:, 0], table[:].rearrange("p k c -> p (k c)"))
            for par in range(2):
                nc.vector.tensor_copy(values_hl[par][:, :, 0:2], token_at.unsqueeze(2).broadcast_to([P, TB, 2]))
            link(nc.vector.tensor_copy(e_str[:], e_raw[:]))
            nc.vector.tensor_tensor(table_hl[:, 1], table[:].rearrange("p k c -> p (k c)"), table_hl[:, 0], ALU.subtract)
            nc.vector.tensor_copy(e_swp[64:128, :], e_raw[64:128, :])
            nc.vector.tensor_tensor(e_swp[0:64, :], e_raw[0:64, :], e_str[0:64, :], ALU.subtract)
            for lo, n in ((2 * P, NA), (NA + 2 * P, NA + NB_), (NA + NB_, NA + NB_ + ND)):
                nc.vector.tensor_tensor(e_str[64:128, lo:n], e_raw[64:128, lo:n], e_str[64:128, lo:n], ALU.subtract)
            nc.vector.tensor_scalar(wg[:], wi_v[:, 0], W_SCALE, None, ALU.mult)
            nc.vector.tensor_scalar(wu[:], wi_v[:, 1], W_SCALE, None, ALU.mult)
            nc.vector.tensor_scalar(wd[:], wi_v[:, 2].rearrange("p (h d) -> p h d", h=HC), W_SCALE, None, ALU.mult)\
              .then_inc(s_prep_w, 1)

            def dve_fori(links):
                return lambda lo, hi, body: loop(lo, hi, links, body)

            dve.wait_ge(s_rstd, 2)

            def ln1(n, par):
                if later(n):
                    dve.wait_ge(s_xT, n - 1)
                first_norm(n, par).then_inc(s_xn, 1)
            pairs(dve_fori(2), ln1)

            dve.wait_ge(s_ex, 1)
            link(nc.vector.tensor_scalar_add(tk_val, tk_work, 1.0))
            link(nc.vector.reciprocal(tk_val, tk_val))
            link(nc.vector.tensor_copy(tk_work, tk_val))

            def best8(n):
                link(nc.vector.max(tk_m8, tk_work))
                carry()
                link(nc.vector.match_replace(tk_work, tk_m8, tk_work, -1.0))
            loop(0, KSEL // 8, 2, best8)
            link(nc.vector.tensor_tensor(tk_mask, tk_work, tk_val, ALU.is_lt))
            link(nc.vector.tensor_tensor_scan(tk_pos, ones[0:E * B, :], tk_mask, 0.0, ALU.mult, ALU.add))
            nc.vector.tensor_tensor(tk_rank, tk_pos, tk_mask, ALU.mult).then_inc(s_tk, 1)

            rank_of, value_of = (rvT[:, a].rearrange("p k (e b) -> p k e b", e=E) for a in range(2))

            dve.wait_ge(s_rv, 1)

            def gather(n, par):
                if later(n):
                    dve.wait_ge(s_gath, n - 1)
                nc.vector.tensor_copy(values_hl[par][:, :, 2:2 + E], value_of[:, :, :, n])
                nc.vector.tensor_copy(rk_s[:, par], rank_of[:, :, :, n])
                link(first_norm(n, par))
                xn = xn_g[:, par].rearrange("p k d -> p (k d)")
                link(nc.vector.tensor_copy(xn_hl[:, par, 0], xn))
                nc.vector.tensor_tensor(xn_hl[:, par, 1], xn, xn_hl[:, par, 0], ALU.subtract)
                nc.vector.tensor_tensor(values_hl[par][:, :, 2 + E:], value_of[:, :, :, n], values_hl[par][:, :, 2:2 + E], ALU.subtract)
                for k in range(TB):
                    ins = nc.vector.tensor_tensor(sels[par][:, k].rearrange("p (e q) -> p e q", e=E),
                                                  rk_s[:, par, k].unsqueeze(2).broadcast_to([P, E, KSEL]),
                                                  iota1.unsqueeze(1).broadcast_to([P, E, KSEL]), ALU.is_equal)
                ins.then_inc(s_sel, 1)
            pairs(dve_fori(6), gather)
            dve.wait_ge(s_gx, B)

            def expert_rows(n, par, m):
                dve.wait_ge(s_yd, n + 1)
                if after_first(m):
                    dve.wait_ge(s_ymv[par], m * 32)
                nc.vector.tensor_tensor(y_s[:, par], bank[7][:].rearrange("p (a m) -> p a m", a=TB),
                                        rinv.unsqueeze(2).broadcast_to([P, TB, P]), ALU.mult).then_inc(s_ys, 1)

            def expert(n, par, m):
                cg = csg[0:64, n].rearrange("p b q -> p (b q)")
                sg = csg[64:128, n].rearrange("p b q -> p (b q)")
                dve.wait_ge(s_q3, n + 1)
                if after_first(n):
                    dve.wait_ge(s_sc, n)
                nc.vector.tensor_tensor(t2q[0:64], bank[2][0:64], sg, ALU.mult)
                nc.vector.tensor_tensor(t2k[0:64], bank[2][64:128], sg, ALU.mult)
                nc.vector.tensor_tensor(qf[0:64], bank[0][0:64], cg, ALU.mult)
                link(nc.vector.tensor_tensor(kf[0:64], bank[1][0:64], cg, ALU.mult))
                nc.vector.tensor_tensor(qf[0:64], qf[0:64], t2q[0:64], ALU.add)
                nc.vector.tensor_tensor(kf[0:64], kf[0:64], t2k[0:64], ALU.add).then_inc(s_rope, 1)
                if after_first(n):
                    dve.wait_ge(s_pexp, n)
                    link(nc.vector.reciprocal(rinv[:], rsum[:]))
                    dve.wait_ge(s_pt, n)
                dve.wait_ge(s_sc, n + 1)
                link(nc.vector.scalar_tensor_tensor(s1[:], bank[4][:].rearrange("p (a m) -> p a m", a=TB), float(P) ** -0.5,
                                                    causal.unsqueeze(1).broadcast_to([P, TB, P]), ALU.mult, ALU.add))
                link(nc.vector.tensor_reduce(nmax[:], s1[:], AX.X, ALU.max))
                nc.vector.tensor_scalar(nmax[:], nmax[:], -1.0, None, ALU.mult).then_inc(s_sm, 1)
                if after_first(n):
                    expert_rows(n - 1, 1 - par, m if par else m - 1)

            expert(0, 0, 0)
            expert(1, 1, 0)
            loop(1, E // 2, 8, lambda m: [expert(m * 2 + par, par, m) for par in range(2)])
            dve.wait_ge(s_pexp, E)
            dve.wait_ge(s_ys, E - 1)
            link(nc.vector.reciprocal(rinv[:], rsum[:]))
            expert_rows(E - 1, 1, E // 2 - 1)

            dve.wait_ge(s_ymv[0], 32 * (E // 2))
            dve.wait_ge(s_ymv[1], 32 * (E // 2))

            def weights_back(n, par):
                mine = picks[:, n].rearrange("p (c s) -> p c s", s=NPICK)
                if later(n):
                    dve.wait_ge(s_scat, n - 1)
                nc.vector.tensor_copy(iv_s[:, par, 0], mine[:, :, 0])
                for h in range(2):
                    rows = slice(64 * h, 64 * h + 64)
                    high, low = (picks[rows, n, base:base + (E // 2 - 1) * (NPICK + 2) + 1:NPICK + 2] for base in (2 + h, 2 + E + h))
                    ins = nc.vector.tensor_tensor(iv_s[rows, par, 1], high, low, ALU.add)
                link(ins)
                for e2 in range(E // 2):
                    ins = nc.vector.tensor_scalar(selT[:, par, e2], tokens[:], iv_s[:, par, 0, e2:e2 + 1], iv_s[:, par, 1, e2:e2 + 1],
                                                  ALU.is_equal, ALU.mult)
                ins.then_inc(s_selw, 1)

            def add_experts(n, par):
                dve.wait_ge(s_scat, n + 1)
                nc.vector.tensor_tensor(x_all[:, n], bank[par][:].rearrange("p (k d) -> p k d", k=TB), x_all[:, n],
                                        ALU.add).then_inc(s_ffn, 1)
            lagged(dve_fori(2), weights_back, add_experts)

            dve.wait_ge(s_ffn, B)
            nc.vector.memset(bs6[64:128], 1.0)

            def split(raw, stk, par):
                nc.vector.tensor_copy(stk[0:64, par, 0], raw[0:64])
                link(nc.vector.tensor_copy(stk[64:128, par, 1], raw[64:128]))
                nc.vector.tensor_tensor(stk[64:128, par, 0], raw[0:64], stk[0:64, par, 0], ALU.subtract)
                return nc.vector.tensor_tensor(stk[0:64, par, 1], raw[64:128], stk[64:128, par, 1], ALU.subtract)

            def prep_u(g, q, par):
                dve.wait_ge(s_prep_free, prep_index(g, 1) + 1)
                if q is not None:
                    dve.wait_ge(s_f, (q - 1) * 16)
                split(u_raw, u_stk, par).then_inc(s_us, 1)

            def prep_v(g, par):
                dve.wait_ge(s_prep_free, prep_index(g, 2) + 1)
                link(split(v_raw, v_stk, par))
                nc.vector.tensor_copy(v_swp[0:64, par], v_stk[64:128, par])
                nc.vector.tensor_copy(v_swp[64:128, par], v_stk[0:64, par]).then_inc(s_vs_rdy, 1)

            def add_g(i, j):
                g = i * 8 + j
                dve.wait_ge(s_prep_full, prep_index(g, 0) + 1)
                nb = i if j else i - 1
                nc.vector.scalar_tensor_tensor(x_all[:, nb], prep_bank[:].rearrange("p (k d) -> p k d", k=TB),
                                               0.5 * FACTOR_SCALE ** 2, x_all[:, nb], ALU.mult, ALU.add).then_inc(s_prep_free, 1)

            def evac_o(g, j, o, k):
                dve.wait_ge(s_out, g * 8 + 4 * (o + 1))
                if k is not None:
                    dve.wait_ge(s_prep_full, k)
                nc.vector.tensor_scalar(o_s[j % 2][:, o], o_bank[o][:], sums[:, o, j % 2:j % 2 + 1], None, ALU.add)\
                  .then_inc(s_oe, 1)

            def split2(src, stk):
                link(nc.vector.tensor_copy(stk[:], src[:]))
                nc.vector.tensor_tensor(stk[64:128], src[64:128], stk[64:128], ALU.subtract).then_inc(s_stk, 1)

            def l1(step, L):
                kind, f = step
                s = L * NL + STEP_AT[step]
                if kind == "norm":
                    link(variances(L, mv_s))
                    nc.vector.tensor_scalar(ve[:], mv_s[:, :, 1], EPS, None, ALU.add).then_inc(s_stats2, 1)
                    dve.wait_ge(s_rstd2, L + 1)
                    normalised(xn_s, L, mv_s[:, :, 0:1], rstd_s[:].unsqueeze(2)).then_inc(s_xn2, 1)
                elif kind in "kq" and kind != "":
                    nth = L * 2 + (1 if kind == "k" else 2)
                    dve.wait_ge(s_lf, s + 1)
                    nc.vector.tensor_scalar(kmin[:], l1_bank[:], 0.0, None, ALU.min).then_inc(s_min, 1)
                    dve.wait_ge(s_exp, nth)
                    nc.vector.scalar_tensor_tensor(kf32[:], l1_bank[:], 0.0, kexp[:], ALU.max, ALU.add).then_inc(s_le, 1)
                    dve.wait_ge(s_le, s + 1)
                    split2(kf32, k_stk if kind == "k" else q_stk)
                elif kind == "v":
                    dve.wait_ge(s_le, s + 1)
                    split2(kf32, vl_stk)
                elif kind == "A":
                    dve.wait_ge(s_lf, s + 1)
                    nc.vector.tensor_tensor(ab[:], l1_bank[:], (bs6 if f == NF - 1 else bs)[:], ALU.mult).then_inc(s_le, 1)
                    dve.wait_ge(s_le, s + 1)
                    link(nc.vector.tensor_tensor_scan(pre[:], ones[:], ab[:], 0.0, ALU.mult, ALU.add))
                elif kind in "CD":
                    r, half = round_of(kind, f)
                    dve.wait_ge(s_lf, s + 1)
                    if kind == "C" and f != 1:
                        dve.wait_ge(s_y, L * ROUNDS + max(r - 1, 0))
                    nc.vector.tensor_tensor(pc[half][:, r % 2], l1_bank[:], pre[:], ALU.mult).then_inc(s_le, 1)
                elif kind == "den":
                    dve.wait_ge(s_lf, s + 1)
                    nc.vector.tensor_scalar(small[:, 0:TB], l1_bank[:, 0:TB], 1e-6, None, ALU.max).then_inc(s_le, 1)
                    dve.wait_ge(s_le, s + 1)
                    link(nc.vector.reciprocal(small[:, TB:2 * TB], small[:, 0:TB]))
                    dve.wait_ge(s_yo, L + 1)
                    for k in range(TB):
                        ins = nc.vector.scalar_tensor_tensor(x_all[:, L, k], y_bank[:, k * P:(k + 1) * P], small[:, TB + k:TB + k + 1],
                                                             x_all[:, L, k], ALU.mult, ALU.add)
                    ins.then_inc(s_yfree, 1)
                elif kind == "gate":
                    dve.wait_ge(s_tanh, L * HC + f + 1)
                    nc.vector.scalar_tensor_tensor(gated[:], tg[:], 1.0, l1_bank[:], ALU.add, ALU.mult).then_inc(s_le, 1)
                elif kind == "up":
                    dve.wait_ge(s_lf, s + 1)
                    dve.wait_ge(s_le, s)
                    nc.vector.scalar_tensor_tensor(hid[:, f], gated[:], 0.5, l1_bank[:], ALU.mult, ALU.mult).then_inc(s_le, 1)
                elif kind == "down":
                    dve.wait_ge(s_lf, s + 1)
                    dve.wait_ge(s_yfree, L + 1)
                    nc.vector.tensor_tensor(x_all[:, L], l1_bank[:].rearrange("p (k d) -> p k d", k=TB), x_all[:, L],
                                            ALU.add).then_inc(s_le, 1)

            prep_u(-1, None, 0)
            prep_v(-1, 0)

            def iteration(i, attn, second):
                steps = iter(L1_STEPS if second else [])
                if not attn:
                    add_g(i, 0)
                    dve.wait_ge(s_prep_free, prep_index(i * 8, 0) + 1)
                    for st in steps:
                        l1(st, i - 1)
                    return
                for j in range(PAIRS):
                    g = i * 8 + j
                    for u in range(UNITS):
                        if j * UNITS + u >= L1_FIRST_SLOT:
                            if j == 0 and u == L1_FIRST_SLOT and second:
                                dve.wait_ge(s_prep_free, prep_index(g, 0) + 1)
                            for st in [s for s in [next(steps, None)] if s]:
                                l1(st, i - 1)
                        if u == 1 and (second or j):
                            add_g(i, j)
                        if u == 2:
                            prep_u(g, g + 1 if second or j else None, (j + 1) % 2)
                        if u == 3:
                            prep_v(g, (j + 1) % 2)
                        if u % TB == TB - 1:
                            evac_o(g, j, u // TB, prep_index(g - 1, 0) + 1 if second or j >= 2 else None)
                for st in steps:
                    l1(st, i - 1)

            iteration(0, True, False)
            links = [0]

            def body(i):
                iteration(i, True, True)
            loop(1, B, 3 * PAIRS + 2 + 3 + NF + 1, body)
            iteration(B, False, True)

        @block.scalar
        def _(act):
            def copy(dst, src):
                return nc.scalar.activation(dst, src, ACT.Copy)

            def transposed(n, par):
                act.wait_ge(s_xT, n + 1)
                copy(xn1T[:, n], bank[par][:]).then_inc(s_xnT, 1)

            def logits(n, par):
                act.wait_ge(s_lg, n + 1)
                copy(lg8[0:E, n], bank[2 + par][0:E]).then_inc(s_lgc, 1)
            lagged(fori_of(act), transposed, logits)
            act.wait_ge(s_lgd, 16)
            nc.scalar.activation(tk_work, lg[0:E * B], ACT.Exp, scale=-1.0).then_inc(s_ex, 1)
            act.wait_ge(s_tkT, 1)
            copy(rvT[:].rearrange("p a k c -> p (a k c)"), bank[2][:]).then_inc(s_rv, 1)

            def picked(n, par):
                act.wait_ge(s_gath, n + 1)
                copy(xgT[:, :, n, :], bank[par][:].rearrange("p (e q) -> p e q", e=E))
                copy(csg[:, :, n, :], bank[2 + par][:].rearrange("p (e q) -> p e q", e=E))
                copy(picks[:, n], bank[4 + par][:, 0:(E // 2) * NPICK]).then_inc(s_gx, 1)
            pairs(fori_of(act), picked)

            def picked_rows(n):
                copy(xg_s[:], xgT[:, n].rearrange("p b q -> p (b q)")).then_inc(s_xgs, 1)

            def attended(n, first):
                act.wait_ge(s_pt, n + 1)
                if not first:
                    act.wait_ge(s_av, n)
                copy(ptT[:].rearrange("p a m -> p (a m)"), bank[5][:]).then_inc(s_ptc, 1)
                act.wait_ge(s_av, n + 1)
                if not first:
                    act.wait_ge(s_yd, n)
                copy(avT[:].rearrange("p a m -> p (a m)"), bank[6][:]).then_inc(s_avc, 1)

            def expert(n, par):
                act.wait_ge(s_q3, n + 1)
                if after_first(n):
                    act.wait_ge(s_sc, n)
                copy(qf[64:128], bank[0][64:128])
                copy(kf[64:128], bank[1][64:128]).then_inc(s_qk_hi, 1)
                if after_first(n):
                    attended(n - 1, not later(n))
                act.wait_ge(s_vd, n + 1)
                copy(v_s[:].rearrange("p a m -> p (a m)"), bank[3][:]).then_inc(s_vs, 1)
                if not (isinstance(n, int) and n == E - 1):
                    picked_rows(n + 1)
                act.wait_ge(s_sm, n + 1)
                for a in range(TB):
                    ins = nc.scalar.activation(s1[:, a], s1[:, a], ACT.Exp, bias=nmax[:, a:a + 1], accum_out=rsum[:, a:a + 1])
                ins.then_inc(s_pexp, 1)

            act.wait_ge(s_gx, B)
            picked_rows(0)
            pairs(fori_of(act), expert, 2)
            attended(E - 1, False)

            act.wait_ge(s_ffn, B)

            def prep_raw(g, k, raw, total, par, q):
                act.wait_ge(s_prep_full, prep_index(g, k) + 1)
                if not (isinstance(g, int) and g < 0):
                    act.wait_ge(s_us if k == 1 else s_vs_rdy, g + 1)
                    act.wait_ge(s_prep_full, 4 if isinstance(g, int) and g == 0 else prep_index(g, 0))
                if q is not None:
                    act.wait_ge(s_oe, (q - 1) * 2)
                nc.scalar.activation(raw[:], prep_bank[:], ACT.Copy, accum_out=total[:, par:par + 1]).then_inc(s_prep_free, 1)

            def prep_tok(g, k, tok, par, q):
                act.wait_ge(s_prep_full, prep_index(g, k) + 1)
                if q is not None:
                    act.wait_ge(s_out, (q - 1) * 8)
                copy(tok[:, par].rearrange("p k c -> p (k c)"), prep_bank[:]).then_inc(s_prep_free, 1)

            def tanh_unit(i, n0):
                for n in (n0, n0 + 1):
                    act.wait_ge(s_f, i * 128 + n + 1)
                    if n0 >= 4:
                        act.wait_ge(s_out, i * 64 + n0 // 2 - 1)
                    elif not isinstance(i, int):
                        act.wait_ge(s_out, i * 64 + n0 // 2 - 1)
                    nc.scalar.activation(th[:, n % TH_SLOTS], f_bank[n % F_BANKS][:], ACT.Tanh,
                                         scale=0.5 * FACTOR_SCALE ** 2).then_inc(s_th, 1)

            def l1(step, L):
                kind, f = step
                s = L * NL + STEP_AT[step]
                if kind == "norm":
                    act.wait_ge(s_lf, s + 1)
                    copy(xn2T[:], l1_bank[:]).then_inc(s_le, 1)
                elif kind in "kq" and kind != "":
                    nth = L * 2 + (1 if kind == "k" else 2)
                    act.wait_ge(s_min, nth)
                    nc.scalar.activation(kexp[:], kmin[:], ACT.Exp).then_inc(s_exp, 1)
                elif kind == "v":
                    act.wait_ge(s_lf, s + 1)
                    act.wait_ge(s_stk, L * 3 + 2)
                    copy(kf32[:], l1_bank[:]).then_inc(s_le, 1)
                elif kind == "B":
                    act.wait_ge(s_lf, s + 1)
                    if f == NF - 1:
                        copy(bs6[0:64], l1_bank[0:64]).then_inc(s_le, 1)
                    else:
                        copy(bs[:], l1_bank[:]).then_inc(s_le, 1)
                elif kind == "den":
                    act.wait_ge(s_y, L * ROUNDS + ROUNDS)
                    copy(y_sb[:], y_bank[:]).then_inc(s_ysb, 1)
                elif kind == "gate":
                    act.wait_ge(s_lf, s + 1)
                    act.wait_ge(s_le, s)
                    nc.scalar.activation(tg[:], l1_bank[:], ACT.Tanh, scale=0.5).then_inc(s_tanh, 1)

            prep_raw(-1, 1, u_raw, sums[:, 1], 0, None)
            prep_raw(-1, 2, v_raw, sums[:, 0], 0, None)
            prep_tok(-1, 3, u_tok, 0, None)
            prep_tok(-1, 4, v_tok, 0, None)

            def iteration(i, attn, second):
                steps = iter(L1_STEPS if second else [])
                if attn:
                    tanh_unit(i, 0)
                    for j in range(PAIRS):
                        g = i * 8 + j
                        q = g + 1
                        for u in range(UNITS):
                            if j * UNITS + u < PAIRS * UNITS - 1:
                                tanh_unit(i, 2 * (j * UNITS + u + 1))
                            q1 = q if second or j else None
                            if u == 2:
                                prep_raw(g, 1, u_raw, sums[:, 1], (j + 1) % 2, q1)
                            if u == 3:
                                prep_raw(g, 2, v_raw, sums[:, 0], (j + 1) % 2, q1)
                            if u == 5:
                                prep_tok(g, 3, u_tok, (j + 1) % 2, q1)
                            if u == 6:
                                prep_tok(g, 4, v_tok, (j + 1) % 2, q1)
                            if j * UNITS + u >= L1_FIRST_SLOT:
                                for st in [s for s in [next(steps, None)] if s]:
                                    l1(st, i - 1)
                for st in steps:
                    l1(st, i - 1)

            iteration(0, True, False)
            with act.Fori(1, B) as i:
                iteration(i, True, True)
            iteration(B, False, True)

        @block.tensor
        def _(pe):
            def mm(out, lhsT, rhs, start=True, stop=True):
                return nc.tensor.matmul(out, lhsT, rhs, start=start, stop=stop)

            pe.wait_ge(s_const, 16 * (len(consts) + len(phase_consts)))
            def transposes(n, par):
                pe.wait_ge(s_xn, n + 1)
                if later(n):
                    pe.wait_ge(s_xnT, n - 1)
                for k in range(TB):
                    ins = nc.tensor.transpose(bank[par][:, k * P:(k + 1) * P], xn_g[:, par, k], ident[:])
                ins.then_inc(s_xT, 1)

            def logits(n, par):
                pe.wait_ge(s_xnT, n + 1)
                if later(n):
                    pe.wait_ge(s_lgc, n - 1)
                mm(bank[2 + par][0:E], wr_w[:], xn1T[:, n]).then_inc(s_lg, 1)
            lagged(fori_of(pe), transposes, logits)
            pe.wait_ge(s_lgc, B)
            pe.wait_ge(s_tk, 1)
            for a, src in enumerate((tk_rank, tk_val)):
                for k in range(TB):
                    ins = nc.tensor.transpose(bank[2][:, (a * TB + k) * 64:(a * TB + k + 1) * 64], src[:, k * P:(k + 1) * P],
                                              ident[0:64, 0:64])
            ins.then_inc(s_tkT, 1)
            pe.wait_ge(s_rv, 1)

            def gather(n, par):
                pe.wait_ge(s_sel, n + 1)
                if later(n):
                    pe.wait_ge(s_gx, n - 1)
                for out, parts in ((bank[par], xn_hl[:, par]), (bank[2 + par], table_hl)):
                    for k in range(TB):
                        for h in range(2):
                            mm(out[:], parts[:, h, k * P:(k + 1) * P], sels[par][:, k], k == h == 0, k == TB - 1 and h == 1)
                for e2 in range(E // 2):
                    for k in range(TB):
                        ins = mm(bank[4 + par][:, e2 * NPICK:(e2 + 1) * NPICK], sels[par][:, k, e2 * P:(e2 + 1) * P],
                                 values_hl[par][:, k], k == 0, k == TB - 1)
                ins.then_inc(s_gath, 1)
            pairs(fori_of(pe), gather)
            pe.wait_ge(s_gx, B)

            def attend(n, par, m, first):
                pe.wait_ge(s_pexp, n + 1)
                if not first:
                    pe.wait_ge(s_ptc, n)
                for a in range(TB):
                    ins = nc.tensor.transpose(bank[5][:, a * P:(a + 1) * P], s1[:, a], ident[:])
                ins.then_inc(s_pt, 1)
                pe.wait_ge(s_ptc, n + 1)
                pe.wait_ge(s_vs, n + 1)
                if not first:
                    pe.wait_ge(s_avc, n)
                for a in range(TB):
                    ins = mm(bank[6][:, a * P:(a + 1) * P], v_s[:, a], ptT[:, a])
                ins.then_inc(s_av, 1)

            def expert_out(n, par, m, first):
                pe.wait_ge(s_avc, n + 1)
                pe.wait_ge(s_wo[par], m * 16 + 16)
                if not first:
                    pe.wait_ge(s_ys, n)
                for a in range(TB):
                    ins = mm(bank[7][:, a * P:(a + 1) * P], avT[:, a], wo_e[:, par])
                ins.then_inc(s_yd, 1)

            def expert(n, par, m):
                w = we[:, par]
                xg = xgT[:, n].rearrange("p b q -> p (b q)")
                before = (n - 1, 1 - par, m if par else m - 1, not later(n))
                pe.wait_ge(s_we[par], m * 16 + 16)
                if after_first(n):
                    pe.wait_ge(s_rope, n)
                    pe.wait_ge(s_qk_hi, n)
                mm(bank[0][:], w[:, 0:P], xg)
                mm(bank[1][:], w[:, P:2 * P], xg)
                mm(bank[2][:], w[:, 2 * P:3 * P], xg).then_inc(s_q3, 1)
                if after_first(n):
                    pe.wait_ge(s_vs, n)
                pe.wait_ge(s_xgs, n + 1)
                for a in range(TB):
                    ins = mm(bank[3][:, a * P:(a + 1) * P], xg_s[:, a * P:(a + 1) * P], w[:, 3 * P:4 * P])
                ins.then_inc(s_vd, 1)
                if after_first(n):
                    attend(*before)
                pe.wait_ge(s_rope, n + 1)
                pe.wait_ge(s_qk_hi, n + 1)
                if after_first(n):
                    pe.wait_ge(s_sm, n)
                for a in range(TB):
                    ins = mm(bank[4][:, a * P:(a + 1) * P], qf[:, a * P:(a + 1) * P], kf[:, a * P:(a + 1) * P])
                ins.then_inc(s_sc, 1)
                if after_first(n):
                    expert_out(*before)

            expert(0, 0, 0)
            expert(1, 1, 0)
            with pe.Fori(1, E // 2) as m:
                for par in range(2):
                    expert(m * 2 + par, par, m)
            attend(E - 1, 1, E // 2 - 1, False)
            expert_out(E - 1, 1, E // 2 - 1, False)

            pe.wait_ge(s_ymv[0], 16 * E)
            pe.wait_ge(s_ymv[1], 16 * E)

            def scatter(n, par):
                pe.wait_ge(s_selw, n + 1)
                if later(n):
                    pe.wait_ge(s_ffn, n - 1)
                for k in range(TB):
                    for e2 in range(E // 2):
                        ins = mm(bank[par][:, k * P:(k + 1) * P], selT[:, par, e2, k * P:(k + 1) * P], y_all[:, n, e2],
                                 e2 == 0, e2 == E // 2 - 1)
                ins.then_inc(s_scat, 1)
            pairs(fori_of(pe), scatter)

            pe.wait_ge(s_ffn, B)
            pe.wait_ge(s_prep_w, 1)
            pe.wait_ge(s_ones, 2)

            def prep(g, k, j, i_next):
                n = prep_index(g, k)
                pe.wait_ge(s_prep_free, n)
                if k in (1, 2):
                    ins = mm(prep_bank[:], (uT_w if k == 1 else vT_w)[:, j * P:(j + 1) * P], xn1T[:, i_next])
                else:
                    if k == 3:
                        pe.wait_ge(s_prep_free, prep_index(g, 2) + 1)
                    for t in range(TB):
                        ins = nc.tensor.transpose(prep_bank[:, t * P:(t + 1) * P], (u_raw if k == 3 else v_raw)[:, t * P:(t + 1) * P],
                                                  ident[:])
                ins.then_inc(s_prep_full, 1)

            def project(g, j):
                pe.wait_ge(s_prep_free, prep_index(g, 0))
                pe.wait_ge(s_oe, g * 2)
                was = (j - 1) % PAIRS
                for t in range(TB):
                    for o, w in enumerate((u_w, v_w)):
                        ins = mm(prep_bank[:, t * P:(t + 1) * P], o_s[was % 2][:, o, t * P:(t + 1) * P], w[:, was], o == 0, o == 1)
                ins.then_inc(s_prep_full, 1)

            def scores(i, un):
                j, u = un // UNITS, un % UNITS
                par, o, blk = j % 2, u // TB, u % TB
                if u == 0:
                    pe.wait_ge(s_us, i * PAIRS + j + 1)
                    pe.wait_ge(s_vs_rdy, i * PAIRS + j + 1)
                for h in range(2):
                    n = 2 * un + h
                    if n >= F_BANKS:
                        pe.wait_ge(s_th, i * 128 + n - F_BANKS + 1)
                    elif not isinstance(i, int):
                        pe.wait_ge(s_th, i * 128 - (1, 0, 2)[n])
                    bk = f_bank[n % F_BANKS]
                    cols = slice(blk * P, (blk + 1) * P)
                    if o == 0:
                        mm(bk[:], v_stk[:, par, h, cols], u_stk[:, par, h], True, False)
                        ins = mm(bk[:], v_swp[:, par, h, cols], u_stk[:, par, h], False, True)
                    else:
                        mm(bk[:], u_stk[:, par, h, cols], v_stk[:, par, h], True, False)
                        ins = mm(bk[:], u_stk[:, par, h, cols], v_swp[:, par, h], False, True)
                    ins.then_inc(s_f, 1)

            def weighted(i, un, first_batch):
                j, u = un // UNITS, un % UNITS
                par, o, blk = j % 2, u // TB, u % TB
                g = i * PAIRS + j
                if u == 0:
                    pe.wait_ge(s_prep_free, 4 if first_batch and j == 0 else prep_index(g - 1, 4) + 1)
                if blk == 0 and not (first_batch and j == 0):
                    pe.wait_ge(s_oe, g * 2 - 1 + o)
                pe.wait_ge(s_th, i * 128 + 2 * un + 2)
                tok = (v_tok, u_tok)[o]
                for h in range(2):
                    rows = slice(64 * h, 64 * h + 64)
                    ins = mm(o_bank[o][rows], tok[:, par, blk, rows], th[:, (2 * un + h) % TH_SLOTS], blk == 0, blk == TB - 1)
                ins.then_inc(s_out, 1)

            def spread(step, f):
                at0 = E_AT[step] + f * P
                src = {"A": k_stk, "B": vl_stk, "C": q_stk, "D": q_stk}[step]
                ins = mm(l1_bank[:], e_str[:, at0:at0 + P], src[:], True, f < 2)
                if f >= 2:
                    ins = mm(l1_bank[:], e_swp[:, at0:at0 + P], src[:], False, True)
                return ins

            def y_round(r, L):
                pe.wait_ge(s_le, L * NL + STEP_AT[("C", 1) if r == 0 else ("D", r + 1)] + 1)
                if r == 0:
                    pe.wait_ge(s_yfree, L)
                mm(y_bank[0:64], top_w[:, r], pc[0][:, r % 2], r == 0, r == ROUNDS - 1)
                mm(y_bank[64:128], bot_w[:, r], pc[1][:, r % 2], r == 0, r == ROUNDS - 1).then_inc(s_y, 1)

            def l1(step, L):
                kind, f = step
                s = L * NL + STEP_AT[step]
                if kind == "A" and f >= 2:
                    y_round(f - 2, L)
                if kind == "den":
                    y_round(ROUNDS - 1, L)
                if kind == "norm":
                    pe.wait_ge(s_xn2, L + 1)
                if kind == "B" and f == 0:
                    pe.wait_ge(s_stk, L * 3 + 3)
                pe.wait_ge(s_le, s)
                if kind == "norm":
                    for t in range(TB):
                        ins = nc.tensor.transpose(l1_bank[:, t * P:(t + 1) * P], xn_s[:, t], ident[:])
                elif kind in ("k", "q", "v"):
                    ins = mm(l1_bank[:], {"k": kk_w, "q": qq_w, "v": vv_w}[kind][:], xn2T[:])
                elif kind in ("A", "B", "C", "D"):
                    ins = spread(kind, f)
                elif kind == "den":
                    for t in range(TB):
                        ins = mm(l1_bank[:, t:t + 1], pc[0][:, (ROUNDS - 1) % 2, t * P:(t + 1) * P], zsel[:])
                elif kind in ("gate", "up"):
                    ins = mm(l1_bank[:], (wg if kind == "gate" else wu)[:, f * P:(f + 1) * P], xn2T[:])
                elif kind == "down":
                    for t in range(TB):
                        for h in range(HC):
                            ins = mm(l1_bank[:, t * P:(t + 1) * P], hid[:, h, t * P:(t + 1) * P], wd[:, h], h == 0, h == HC - 1)
                ins.then_inc(s_lf, 1)
                if kind == "den":
                    pe.wait_ge(s_ysb, L + 1)
                    for t in range(TB):
                        ins = mm(y_bank[:, t * P:(t + 1) * P], y_sb[:, t * P:(t + 1) * P], wo2[:])
                    ins.then_inc(s_yo, 1)

            for k in range(1, 5):
                prep(-1, k, 0, 0)

            def iteration(i, attn, second):
                steps = iter(L1_STEPS if second else [])
                if not attn:
                    project(i * PAIRS, 0)
                    for st in steps:
                        l1(st, i - 1)
                    return
                scores(i, 0)
                for j in range(PAIRS):
                    g = i * PAIRS + j
                    for u in range(UNITS):
                        un = j * UNITS + u
                        if un < PAIRS * UNITS - 1:
                            scores(i, un + 1)
                        weighted(i, un, not second)
                        if u == 1 and (second or j):
                            project(g, j)
                        if u in (2, 3, 5, 6):
                            prep(g, {2: 1, 3: 2, 5: 3, 6: 4}[u], (j + 1) % PAIRS, i if j < PAIRS - 1 else i + 1)
                        if un >= L1_FIRST_SLOT:
                            for st in [x for x in [next(steps, None)] if x]:
                                l1(st, i - 1)
                for st in steps:
                    l1(st, i - 1)

            iteration(0, True, False)
            with pe.Fori(1, B) as i:
                iteration(i, True, True)
            iteration(B, False, True)


def tables():
    half = NROT // 2
    inv = (np.float32(1.0) / np.float32(10000.0) ** (np.arange(half, dtype=np.float32) * np.float32(2.0) / np.float32(NROT))).astype(np.float32)
    ang = np.arange(T, dtype=np.float32)[:, None] * inv
    cos, sin = np.cos(ang).astype(np.float32), np.sin(ang).astype(np.float32)
    at = np.arange(P)
    same = at[:, None] // KSEL == at[None, :] // KSEL
    seen = same & (at[:, None] >= at[None, :])
    return {
        "table": np.concatenate([cos, cos, -sin, sin], axis=1),
        "causal": np.where(seen, 0.0, MASKED).astype(np.float32),
        "ident": np.eye(P, dtype=np.float32),
        "tokens": np.tile(np.arange(T, dtype=np.float32), (P, 1)),
        "token_at": (np.arange(TB)[None, :] * P + at[:, None]).astype(np.float32),
        "iota1": np.tile(np.arange(1, KSEL + 1, dtype=np.float32), (P, 1)),
        "zsel": (at >= 64).astype(np.float32)[:, None],
    }


def laid_out(x):
    f32 = np.float32
    wqkv, wo = x["L0_ffn_Wqkv"], x["L0_ffn_Wo"]
    turned = np.concatenate([np.arange(32, 64), np.arange(32)])
    wq, wk, wv = wqkv[:, :, 0:P], wqkv[:, :, P:2 * P], wqkv[:, :, 2 * P:]
    we = np.concatenate([wq, wk, wq[:, :, turned], wk[:, :, turned], wv, wo], axis=2)

    eye = np.eye(DH, dtype=f32)
    ea, eb, ed = (np.zeros((DH, NF * P), f32) for _ in range(3))
    top, bot = (np.zeros((NF * P, DH), f32) for _ in range(2))
    f = 0
    for n in range(DH // LEAF):
        for i in range(LEAF):
            for j in range(LEAF):
                ea[:, f], eb[:, f] = eye[:, n * LEAF + i], eye[:, n * LEAF + j]
                top[f] = eye[n * LEAF + i]
                f += 1
    for lv, (bs, r, nodes) in enumerate(LEVELS):
        UL, VR, UR, VL = (x[f"L1_attn_{w}{lv}"] for w in ("UL", "VR", "UR", "VL"))
        for n in range(nodes):
            left = slice(2 * bs * n, 2 * bs * n + bs)
            right = slice(2 * bs * n + bs, 2 * bs * (n + 1))
            for i in range(r):
                for j in range(r):
                    ea[left, f], eb[right, f], ed[left, f] = UL[:, i], VR[:, j], VL[:, i]
                    top[f, left], bot[f, right] = UL[:, i], UR[:, j]
                    f += 1
    ea[:, f:f + DH] = eb[:, f:f + DH] = eye
    assert f + DH == NF * P
    e = np.concatenate([ea, eb, ed[:, 2 * P:]], axis=1)
    tiles = lambda a: a.reshape(NF, P, DH)
    top_w = np.stack([tiles(top)[t] for t in (0, 2, 3, 4, 5, 6)], axis=1)
    bot_w = np.stack([tiles(top)[1]] + [tiles(bot)[t] for t in (2, 3, 4, 5, 6)], axis=1)
    twice = lambda w: np.concatenate([w, w], axis=1)
    wd = x["L1_ffn_w_down"].T.reshape(HC, P, D).transpose(1, 0, 2).reshape(P, HIDDEN)
    return {
        "x": x["L0_attn_qz"],
        "u": x["L0_attn_ternary_factor_u"], "v": x["L0_attn_ternary_factor_v"],
        "uT": x["L0_attn_ternary_factor_u"].T, "vT": x["L0_attn_ternary_factor_v"].T,
        "wrT": x["L0_ffn_Wr"].T, "we": we,
        "wk2": twice(x["L1_attn_Wk"]), "wq2": twice(x["L1_attn_Wq"]), "wv2": twice(x["L1_attn_Wv"]),
        "wo2": np.concatenate([x["L1_attn_Wo"]] * 2, axis=0),
        "top": top_w, "bot": bot_w, "e": np.concatenate([e, e], axis=0),
        "wi": np.stack([x["L1_ffn_w_gate"].T, x["L1_ffn_w_up"].T, wd], axis=1),
    }


def kernel(**inputs):
    import concourse.bacc as bacc
    from concourse.bass_utils import run_bass_kernel_spmd

    nc = bacc.Bacc("TRN2", target_bir_lowering=False, num_devices=1)
    arrays, io = {}, {}
    for name, a in {**laid_out({k: np.asarray(v) for k, v in inputs.items()}), **tables()}.items():
        a = np.ascontiguousarray(a)
        arrays[f"in_{name}"] = a
        io[name] = nc.dram_tensor(f"in_{name}", a.shape, mybir.dt.from_np(a.dtype), kind="ExternalInput").ap()
    io["out"] = nc.dram_tensor("out_0", (B, T, D), F32, kind="ExternalOutput").ap()
    build(nc, io)
    return run_bass_kernel_spmd(nc, [arrays], core_ids=[0]).results[0]["out_0"]
```

```python
from contextlib import ExitStack

import concourse.bass as bass
import numpy as np
from concourse import mybir

F32 = mybir.dt.float32
F32R = mybir.dt.float32r
I32 = mybir.dt.int32
ALU = mybir.AluOpType
ACT = mybir.ActivationFunctionType
AX = mybir.AxisListType

P = 128
B, T, D = 8, 512, 128
TB = T // P
EPS = 1e-5

C, R = 16, 64
PAIRS = C // 2
FACTOR_SCALE = 0.03125

E, KSEL = 8, 64
NROT = 64
EW = 3 * P + 2 * NROT + P
MASKED = -3.0e38
NPICK = 2 + 2 * E

DH, LEAF = 64, 4
LEVELS = [(4, 4, 8), (8, 8, 4), (16, 8, 2), (32, 8, 1)]
NF = 7
ROUNDS = 6
HIDDEN = 384
HC = HIDDEN // P
W_SCALE = 1.0 / 127.0

UNITS = 2 * TB
F_BANKS = 3
TH_SLOTS = 4

L1_STEPS = [("back", 0), ("norm", 0), ("k", 0), ("q", 0), ("v", 0)]
for _f in range(NF):
    L1_STEPS += [("B", _f), ("A", _f), ("C", _f)] + ([("D", _f)] if _f >= 2 else [])
for _h in range(HC):
    L1_STEPS += [("gate", _h), ("up", _h)]
L1_STEPS += [("den", 0), ("down", 0)]
NL = len(L1_STEPS)
STEP_AT = {s: n for n, s in enumerate(L1_STEPS)}
BY_ACT = ("norm", "v", "B")
N_ACT = sum(kind in BY_ACT for kind, _ in L1_STEPS)
N_DVE = NL - N_ACT


def emptied_before(step):
    own = step[0] in BY_ACT
    return sum((kind in BY_ACT) == own for kind, _ in L1_STEPS[:STEP_AT[step] + 1])


L1_STATS_SLOT, L1_ROWS_SLOT = 3, 5
L1_SLOTS = [2, 7, 8, 10, 14] + [n for n in range(16, 8 * 8) if n % 8 not in (4, 5)]


X_PARTS = 4
X_PART = B // X_PARTS


def round_of(kind, f):
    if f < 2:
        return 0, f
    return f - 1, 0 if kind == "C" else 1


def prep_index(g, k):
    return k - 1 if isinstance(g, int) and g < 0 else g * 5 + 3 + k


def build(nc, io):
    ctx = ExitStack()
    with ctx:
        def sb(name, shape, dt=F32):
            return ctx.enter_context(nc.sbuf_tensor(name, shape, dt))

        def sem(name):
            return ctx.enter_context(nc.semaphore(name))

        bank = [ctx.enter_context(nc.psum_tensor(f"bank{n}", [P, 512], F32)) for n in range(8)]
        f_bank = bank[0:F_BANKS]
        o_bank = bank[3:5]
        prep_bank, l1_bank, y_bank = bank[5], bank[6], bank[7]
        last_banks = [l1_bank] + bank[0:6]

        x_all = sb("x_all", [P, B, TB, D])
        xn1T = sb("xn1T", [P, B + 1, T])
        ident = sb("ident", [P, P])
        ones = sb("ones", [P, 512])
        kk_w, qq_w, vv_w = sb("kk_w", [P, P]), sb("qq_w", [P, P]), sb("vv_w", [P, P])
        wo2 = sb("wo2", [P, D])
        top_w, bot_w = sb("top_w", [P, ROUNDS, DH]), sb("bot_w", [P, ROUNDS, DH])
        zsel = sb("zsel", [P, 1])
        wd = sb("wd", [P, HC, D])
        NA, NB_, ND = NF * P, NF * P, (NF - 2) * P
        e_str = sb("e_str", [P, NA + NB_ + ND], F32R)
        e_swp = sb("e_swp", [P, NA + NB_ + ND], F32R)
        E_AT = {"A": 0, "B": NA, "C": NA, "D": NA + NB_ - 2 * P}
        u_stk, v_stk, v_swp = (sb(n, [P, 2, 2, T], F32R) for n in ("u_stk", "v_stk", "v_swp"))
        k_stk, q_stk, vl_stk = (sb(n, [P, T], F32R) for n in ("k_stk", "q_stk", "vl_stk"))
        stats = sb("stats", [P, TB, 6])
        mv_s, rstd_s, ve = sb("mv_s", [P, TB, 2]), sb("rstd_s", [P, TB]), sb("ve", [P, TB])
        mr_s = sb("mr_s", [P, 2, 2, TB])
        mv1, ve1, rstd1 = sb("mv1", [P, B, TB, 2]), sb("ve1", [P, B, TB]), sb("rstd1", [P, B, TB])
        powc = sb("powc", [P, 1])
        sel_r = sb("sel_r", [P, TB, E * KSEL], F32R)
        idle = sb("idle", [P, 1])
        xn_s = sb("xn_s", [P, TB, D])
        sums = sb("sums", [P, 2, 2])
        small = sb("small", [P, 8])

        def view(a, shape):
            if len(shape) == 2:
                return a.rearrange("p (a b) -> p a b", a=shape[0])
            if len(shape) == 3:
                return a.rearrange("p (a b c) -> p a b c", a=shape[0], b=shape[1])
            return a

        ARENA, UPPER = 14848, 6924
        arena = sb("arena", [P, ARENA])
        early = ExitStack()

        def sb_early(name, shape):
            return early.enter_context(nc.sbuf_tensor(name, shape, F32))

        u_w, v_w = sb_early("u_w", [P, PAIRS * D]), sb_early("v_w", [P, PAIRS * D])
        uT_w, vT_w = sb_early("uT_w", [P, C * R]), sb_early("vT_w", [P, C * R])
        wg, wu = sb_early("wg", [P, HIDDEN]), sb_early("wu", [P, HIDDEN])
        upper = sb_early("upper", [P, UPPER])
        at, at_upper = [0], [0]

        def take(*shape):
            n = int(np.prod(shape))
            at[0] += n
            assert at[0] <= ARENA, at[0]
            return view(arena[:, at[0] - n:at[0]], shape)

        def take_upper(*shape):
            n = int(np.prod(shape))
            at_upper[0] += n
            assert at_upper[0] <= UPPER, at_upper[0]
            return view(upper[:, at_upper[0] - n:at_upper[0]], shape)

        xgT = take(E, B, KSEL)
        csg = take(E, B, KSEL)
        y_all = take(B, E // 2, D)
        rvT = take(2, TB, E * B)
        rk_s = take(2, TB, E)
        iota1 = take(KSEL)
        tokens = take(T)
        picks = take(B, (E // 2) * NPICK)
        iv_s = take(2, 2, E // 2)
        token_at = take(TB)
        causal = take(P)
        we, wo_e = take_upper(2, EW - P), take(2, P)
        mark = at_upper[0]
        xg_s = take_upper(T)
        t2q, t2k = take_upper(T), take_upper(T)
        qf, kf = take_upper(T), take_upper(T)
        v_s, s1, ptT, avT = (take_upper(TB, P) for _ in range(4))
        y_s = take_upper(2, TB, P)
        nmax, rsum, rinv = take_upper(TB), take_upper(TB), take_upper(TB)
        at_upper[0] = mark
        wr_w = take_upper(E)
        lg = take_upper(T)
        xn_g = take_upper(2, TB, D)
        stats1 = take_upper(B, TB, 6)
        table = take_upper(TB, P)
        at[0] = E * B * KSEL
        lg8 = take(B, T)
        at[0] = E * B * KSEL
        selT = take(2, E // 2, T)
        sels = [sel_r, v_stk[:].rearrange("p a b t -> p (a b) t")]
        xn_hl = u_stk
        table_hl = v_swp[:, 0]
        values_hl = [v_swp[:, 1, par, 0:TB * NPICK].rearrange("p (k c) -> p k c", k=TB) for par in range(2)]
        tk_val, tk_work, tk_mask, tk_pos, tk_rank = (xgT[0:E * B, e].rearrange("p b k -> p (b k)") for e in range(5))
        tk_m8 = small[0:E * B, 0:8]
        at[0] = 2 * E * B * KSEL
        e_raw = take(NA + NB_ + ND)
        wi = take(3 * HIDDEN).bitcast(I32)
        at[0] = 0
        u_raw, v_raw = take(T), take(T)
        u_tok, v_tok = take(2, TB, P), take(2, TB, P)
        th = take(TH_SLOTS, T)
        o_s = take(2, T)
        gT = take(T)
        xn2T, kmin, kexp, kf32, bs, bs6, ab, pre = (take(T) for _ in range(8))
        y_sb, gated = kmin, ab
        pc = [take(2, T), take(2, T)]
        tg = take(T)
        hid = take(HC, T)
        early.close()
        o_hl = sb("o_hl", [P, 2, 2, T], F32R)
        w_hl = [sb(n, [P, 2, PAIRS * D], F32R) for n in ("u_w_hl", "v_w_hl")]
        uv_hl = [sb(n, [P, 2, C * R], F32R) for n in ("u_hl", "v_hl")]
        gu_hl = [sb(n, [P, 2, HIDDEN], F32R) for n in ("gate_hl", "up_hl")]
        xn1_hl, xn2_hl = sel_r[:, 0:2], sel_r[:, 2:4]

        s_stage, s_const = sem("stage_loaded"), sem("consts_loaded")
        s_x = [sem(f"x_part{n}_loaded") for n in range(X_PARTS)]
        s_first = sem("first_consts_loaded")
        s_hi, s_parts = sem("weights_high"), sem("weight_parts_ready")
        s_x1, s_x2 = sem("xn1_parts_ready"), sem("xn2_parts_ready")
        s_prep_w, s_ones, s_powc = sem("weights_split"), sem("ones_set"), sem("powc_set")
        s_stats, s_rstd = sem("stats_ready"), sem("rstd_ready")
        s_xn, s_xT, s_xnT = sem("xn_ready"), sem("xn_transposed"), sem("xn1T_ready")
        s_lg, s_lgc, s_lgd = sem("logits_done"), sem("logits_copied"), sem("logits_moved")
        s_ex, s_tk, s_tkT, s_rv = sem("router_exp"), sem("topk_done"), sem("topk_transposed"), sem("ranks_ready")
        s_sel, s_gath, s_gx = sem("sel_ready"), sem("gathered"), sem("gather_copied")
        s_we, s_wo = [sem("expert_w0"), sem("expert_w1")], [sem("expert_wo0"), sem("expert_wo1")]
        s_q3, s_rope, s_vd, s_vs = sem("qkr_done"), sem("rope_done"), sem("expert_v_done"), sem("expert_v_copied")
        s_sc, s_sm, s_pexp, s_pt, s_ptc = (sem(n) for n in ("scores_done", "shifted", "probs_ready", "probsT_done", "probsT_copied"))
        s_av, s_avc, s_yd, s_ys = (sem(n) for n in ("av_done", "av_copied", "expert_y_done", "expert_y_scaled"))
        s_ymv = [sem("expert_y_moved0"), sem("expert_y_moved1")]
        s_xg, s_xgh = sem("gather_rows_ready"), sem("gather_rows_high_ready")
        s_qk_hi, s_xgs = sem("qk_passed_rows"), sem("picked_copied")
        s_selw, s_scat, s_ffn = (sem(n) for n in ("selT_ready", "scattered", "ffn_added"))
        s_chain = sem("dve_chain")
        s_prep_full, s_prep_free = sem("prep_bank_full"), sem("prep_bank_free")
        s_us, s_vs_rdy = sem("u_stack_ready"), sem("v_stack_ready")
        s_f, s_th, s_out, s_oe = sem("scores_full"), sem("tanh_done"), sem("unit_done"), sem("o_evacuated")
        s_oh, s_ol = sem("o_high_ready"), sem("o_low_ready")
        s_lf, s_la, s_ld = sem("l1_bank_full"), sem("l1_emptied_by_act"), sem("l1_emptied_by_dve")

        def wait_emptied(engine, step, L):
            if step[0] in BY_ACT:
                engine.wait_ge(s_la, L * N_ACT + emptied_before(step))
            else:
                engine.wait_ge(s_ld, L * N_DVE + emptied_before(step))

        s_stats2, s_rstd2, s_xn2 = sem("l1_stats"), sem("l1_rstd"), sem("l1_xn")
        s_min, s_exp, s_stk, s_tanh = sem("l1_min"), sem("l1_exp"), sem("l1_stack"), sem("l1_tanh")
        s_y, s_ysb, s_yo, s_yfree = sem("l1_y"), sem("l1_y_copied"), sem("l1_y_out"), sem("l1_y_bank_free")
        s_st = sem("stored")

        first_consts = [(ident, io["ident"]), (wr_w, io["wrT"])]
        consts = [(uT_w, io["uT"]), (vT_w, io["vT"]),
                  (u_w[:].rearrange("p (j d) -> p j d", j=PAIRS), io["u"].rearrange("(j p) d -> p j d", p=P)),
                  (v_w[:].rearrange("p (j d) -> p j d", j=PAIRS), io["v"].rearrange("(j p) d -> p j d", p=P)),
                  (kk_w, io["wk2"]), (qq_w, io["wq2"]), (vv_w, io["wv2"]), (wo2, io["wo2"]),
                  (top_w, io["top"]), (bot_w, io["bot"]), (zsel, io["zsel"])]
        phase_consts = [(table, io["table"].rearrange("(k p) c -> p k c", p=P)),
                        (causal, io["causal"]), (iota1, io["iota1"]),
                        (tokens, io["tokens"]), (token_at, io["token_at"])]
        wi_v = wi.rearrange("p (a b) -> p a b", a=3)

        def pairs(fori, body, tail=0):
            for n in range(2):
                body(n, n)
            fori(1, (B - tail) // 2, lambda m: [body(m * 2 + par, par) for par in range(2)])
            for n in range(B - tail, B):
                body(n, n % 2)

        def lagged(fori, first, second):
            def both(n, par):
                first(n + 1, 1 - par)
                second(n, par)
            first(0, 0)
            for n in range(2):
                both(n, n)
            fori(1, B // 2 - 1, lambda m: [both(m * 2 + par, par) for par in range(2)])
            both(B - 2, 0)
            second(B - 1, 1)

        def fori_of(engine):
            def fori(lo, hi, body):
                with engine.Fori(lo, hi) as m:
                    body(m)
            return fori

        def later(n):
            return not (isinstance(n, int) and n < 2)

        def after_first(n):
            return not (isinstance(n, int) and n < 1)

        block = ctx.enter_context(nc.Block())

        @block.sync
        def _(sp):
            for h in range(X_PARTS):
                part = slice(h * X_PART, (h + 1) * X_PART)
                sp.dma_start(x_all[:, part], io["x"][part].rearrange("b (k p) d -> p b k d", p=P)).then_inc(s_x[h], 16)
                if h == 0:
                    for dst, src in first_consts:
                        sp.dma_start(dst[:], src).then_inc(s_first, 16)
            for dst, src in consts + phase_consts:
                sp.dma_start(dst[:], src).then_inc(s_const, 16)
            for par in range(2):
                sp.dma_start(we[:, par], io["we"][par, :, 0:EW - P]).then_inc(s_we[par], 16)
                sp.dma_start(wo_e[:, par], io["we"][par, :, EW - P:EW]).then_inc(s_wo[par], 16)
            sp.wait_ge(s_lgc, B)
            sp.dma_start(lg[0:E * B], lg8[0:E]).then_inc(s_lgd, 16)

            def load_qkv(n, par):
                sp.wait_ge(s_vd, n + 1)
                sp.dma_start(we[:, par], io["we"][n + 2, :, 0:EW - P]).then_inc(s_we[par], 16)

            def load_wo(n, par):
                sp.wait_ge(s_yd, n + 1)
                sp.dma_start(wo_e[:, par], io["we"][n + 2, :, EW - P:EW]).then_inc(s_wo[par], 16)

            sp.wait_ge(s_prep_w, 1)

            def move_rows(n, ep, par):
                sp.wait_ge(s_ys, n + 1)
                for half in range(2):
                    sp.dma_start(y_all[64 * par:64 * par + 64].rearrange("p (q r) e d -> p q r e d", r=2)[:, :, half, ep, :],
                                 y_s[64 * half:64 * half + 64, par]).then_inc(s_ymv[par], 16)

            load_qkv(0, 0)
            load_qkv(1, 1)
            with sp.Fori(0, E // 2 - 2) as m:
                for par in range(2):
                    n = m * 2 + par
                    load_wo(n, par)
                    move_rows(n, m, par)
                    load_qkv(n + 2, par)
            for par in range(2):
                load_wo(E - 4 + par, par)
                move_rows(E - 4 + par, E // 2 - 2, par)
            for par in range(2):
                move_rows(E - 2 + par, E // 2 - 1, par)
            with sp.Fori(0, B) as n:
                sp.wait_ge(s_ld, n * N_DVE + N_DVE)
                sp.dma_start(io["out"][n].rearrange("(k p) d -> p k d", p=P), x_all[:, n]).then_inc(s_st, 16)
            sp.wait_ge(s_st, 16 * B)

        @block.gpsimd
        def _(pool):
            pool.memset(powc[:], -0.5).then_inc(s_powc, 1)
            pool.memset(ones[:], 1.0).then_inc(s_ones, 1)
            pool.memset(xn1T[:, B, :], 0.0).then_inc(s_ones, 1)
            pool.dma_start(e_raw[:, 0:NA + NB_ + ND], io["e"]).then_inc(s_stage, 16)
            pool.dma_start(wi_v[:], io["wi"]).then_inc(s_stage, 16)
            pool.wait_ge(s_powc, 1)
            for h in range(X_PARTS):
                part = slice(h * X_PART, (h + 1) * X_PART)
                pool.wait_ge(s_stats, h + 1)
                pool.tensor_tensor(rstd1[:, part], ve1[:, part], powc[:].unsqueeze(2).broadcast_to([P, X_PART, TB]), ALU.pow)\
                    .then_inc(s_rstd, 1)
            pool.wait_ge(s_stage, 32)
            pool.tensor_copy(e_str[:], e_raw[:]).then_inc(s_hi, 1)
            pool.wait_ge(s_hi, 1)
            pool.tensor_scalar(wg[:], wi_v[:, 0], W_SCALE, None, ALU.mult)
            pool.tensor_scalar(wu[:], wi_v[:, 1], W_SCALE, None, ALU.mult)
            pool.tensor_scalar(wd[:], wi_v[:, 2].rearrange("p (h d) -> p h d", h=HC), W_SCALE, None, ALU.mult).then_inc(s_hi, 1)
            pool.wait_ge(s_hi, 2)
            pool.tensor_copy(e_swp[64:128, :], e_raw[64:128, :]).then_inc(s_hi, 1)
            pool.wait_ge(s_hi, 3)
            pool.tensor_tensor(e_swp[0:64, :], e_raw[0:64, :], e_str[0:64, :], ALU.subtract).then_inc(s_hi, 1)
            pool.wait_ge(s_hi, 4)
            for lo, n in ((2 * P, NA), (NA + 2 * P, NA + NB_), (NA + NB_, NA + NB_ + ND)):
                ins = pool.tensor_tensor(e_str[64:128, lo:n], e_raw[64:128, lo:n], e_str[64:128, lo:n], ALU.subtract)
            ins.then_inc(s_prep_w, 1)
            pool.wait_ge(s_ymv[0], 16 * E)
            pool.wait_ge(s_ymv[1], 16 * E)
            first = ((uT_w, uv_hl[0]), (vT_w, uv_hl[1]), (wg, gu_hl[0]), (wu, gu_hl[1]))
            then = ((u_w, w_hl[0]), (v_w, w_hl[1]))
            for w, parts in first:
                pool.tensor_copy(parts[:, 0], w[:]).then_inc(s_hi, 1)
            pool.wait_ge(s_hi, 4 + len(first))
            for w, parts in first:
                pool.tensor_tensor(parts[:, 1], w[:], parts[:, 0], ALU.subtract).then_inc(s_parts, 1)
            pool.wait_ge(s_parts, len(first))
            pool.wait_ge(s_prep_full, 2)
            for w, parts in then:
                pool.tensor_copy(parts[:, 0], w[:]).then_inc(s_hi, 1)
            pool.wait_ge(s_hi, 4 + len(first) + len(then))
            for w, parts in then:
                pool.tensor_tensor(parts[:, 1], w[:], parts[:, 0], ALU.subtract).then_inc(s_parts, 1)
            with pool.Fori(0, B) as n:
                pool.wait_ge(s_stats2, n + 1)
                pool.tensor_tensor(rstd_s[:], ve[:], powc[:].broadcast_to([P, TB]), ALU.pow).then_inc(s_rstd2, 1)

        @block.vector
        def _(dve):
            chain = [0, 0]

            def link(ins):
                ins.then_inc(s_chain, 1)
                chain[1] += 1
                dve.wait_ge(s_chain, chain[0] + chain[1])

            def carry():
                nc.vector.memset(idle[:], 0.0)

            def loop(lo, hi, links, body):
                first = chain[0] + chain[1]
                with dve.Fori(lo, hi) as n:
                    chain[0], chain[1] = (n - lo if lo else n) * links + first, 0
                    body(n)
                    assert chain[1] == links, chain
                chain[0], chain[1] = first + (hi - lo) * links, 0

            def variances(n, mv):
                carry()
                for k in range(TB):
                    ins = nc.vector.bn_stats(stats[:, k], x_all[:, n, k])
                link(ins)
                carry()
                for k in range(TB):
                    ins = nc.vector.bn_aggr(mv[:, k], stats[:, k])
                return ins

            def normalised(dst, n, mean, inv):
                for k in range(TB):
                    ins = nc.vector.tensor_scalar(dst[:, k], x_all[:, n, k], mean[:, k], inv[:, k],
                                                  ALU.subtract, ALU.mult)
                return ins

            def first_norm(n, par):
                nc.vector.tensor_copy(mr_s[:, par, 0], mv1[:, n, :, 0])
                link(nc.vector.tensor_copy(mr_s[:, par, 1], rstd1[:, n]))
                return normalised(xn_g[:, par], n, mr_s[:, par, 0].unsqueeze(2), mr_s[:, par, 1].unsqueeze(2))

            def part_statistics(h):
                part = slice(h * X_PART, (h + 1) * X_PART)
                dve.wait_ge(s_x[h], 16)
                for n in range(h * X_PART, (h + 1) * X_PART):
                    for k in range(TB):
                        ins = nc.vector.bn_stats(stats1[:, n, k], x_all[:, n, k])
                link(ins)
                for n in range(h * X_PART, (h + 1) * X_PART):
                    for k in range(TB):
                        ins = nc.vector.bn_aggr(mv1[:, n, k], stats1[:, n, k])
                link(ins)
                nc.vector.tensor_scalar(ve1[:, part], mv1[:, part, :, 1], EPS, None, ALU.add).then_inc(s_stats, 1)

            def part_rows(h):
                dve.wait_ge(s_rstd, h + 1)
                for n in range(h * X_PART, (h + 1) * X_PART):
                    if n >= 2:
                        dve.wait_ge(s_xT, n - 1)
                    normalised(xn_g[:, n % 2], n, mv1[:, n, :, 0:1], rstd1[:, n].unsqueeze(2)).then_inc(s_xn, 1)

            part_statistics(0)
            for h in range(1, X_PARTS):
                part_statistics(h)
                part_rows(h - 1)
            part_rows(X_PARTS - 1)

            def dve_fori(links):
                return lambda lo, hi, body: loop(lo, hi, links, body)

            dve.wait_ge(s_const, 16 * (len(consts) + len(phase_consts)))
            link(nc.vector.tensor_copy(table_hl[:, 0], table[:].rearrange("p k c -> p (k c)")))
            for par in range(2):
                nc.vector.tensor_copy(values_hl[par][:, :, 0:2], token_at.unsqueeze(2).broadcast_to([P, TB, 2]))
            nc.vector.tensor_tensor(table_hl[:, 1], table[:].rearrange("p k c -> p (k c)"), table_hl[:, 0], ALU.subtract)

            for n in range(2):
                dve.wait_ge(s_xT, B - 1 + n)
                normalised(xn_g[:, n], n, mv1[:, n, :, 0:1], rstd1[:, n].unsqueeze(2)).then_inc(s_xg, 1)

            dve.wait_ge(s_ex, 1)
            link(nc.vector.tensor_scalar_add(tk_val, tk_work, 1.0))
            link(nc.vector.reciprocal(tk_val, tk_val))

            for n in range(KSEL // 8):
                left = tk_work if n else tk_val
                link(nc.vector.max(tk_m8, left))
                link(nc.vector.match_replace(tk_work, tk_m8, left, -1.0))
            link(nc.vector.tensor_tensor(tk_mask, tk_work, tk_val, ALU.is_lt))
            link(nc.vector.tensor_tensor_scan(tk_pos, ones[0:E * B, :], tk_mask, 0.0, ALU.mult, ALU.add))
            nc.vector.tensor_tensor(tk_rank, tk_pos, tk_mask, ALU.mult).then_inc(s_tk, 1)

            rank_of, value_of = (rvT[:, a].rearrange("p k (e b) -> p k e b", e=E) for a in range(2))

            dve.wait_ge(s_rv, 1)

            def gather(n, par):
                if later(n):
                    dve.wait_ge(s_gath, n - 1)
                nc.vector.tensor_copy(values_hl[par][:, :, 2:2 + E], value_of[:, :, :, n])
                ranks = nc.vector.tensor_copy(rk_s[:, par], rank_of[:, :, :, n])
                if later(n):
                    first_norm(n, par).then_inc(s_xg, 1)
                else:
                    link(ranks)
                xn = xn_g[:, par].rearrange("p k d -> p (k d)")
                nc.vector.tensor_tensor(values_hl[par][:, :, 2 + E:], value_of[:, :, :, n], values_hl[par][:, :, 2:2 + E], ALU.subtract)
                for k in range(TB):
                    ins = nc.vector.tensor_tensor(sels[par][:, k].rearrange("p (e q) -> p e q", e=E),
                                                  rk_s[:, par, k].unsqueeze(2).broadcast_to([P, E, KSEL]),
                                                  iota1.unsqueeze(1).broadcast_to([P, E, KSEL]), ALU.is_equal)
                dve.wait_ge(s_xgh, n + 1)
                nc.vector.tensor_tensor(xn_hl[:, par, 1], xn, xn_hl[:, par, 0], ALU.subtract).then_inc(s_sel, 1)
            gather(0, 0)
            gather(1, 1)
            loop(1, B // 2, 2, lambda m: [gather(m * 2 + par, par) for par in range(2)])
            dve.wait_ge(s_gx, B)

            def expert_rows(n, par, m):
                dve.wait_ge(s_yd, n + 1)
                if after_first(m):
                    dve.wait_ge(s_ymv[par], m * 32)
                nc.vector.tensor_tensor(y_s[:, par], bank[7][:].rearrange("p (a m) -> p a m", a=TB),
                                        rinv.unsqueeze(2).broadcast_to([P, TB, P]), ALU.mult).then_inc(s_ys, 1)

            def expert(n, par, m):
                cg = csg[0:64, n].rearrange("p b q -> p (b q)")
                sg = csg[64:128, n].rearrange("p b q -> p (b q)")
                dve.wait_ge(s_q3, n * 3 + 1)
                if after_first(n):
                    dve.wait_ge(s_sc, n)
                nc.vector.tensor_tensor(t2q[0:64], bank[2][0:64], sg, ALU.mult)
                nc.vector.tensor_tensor(t2k[0:64], bank[2][64:128], sg, ALU.mult)
                dve.wait_ge(s_q3, n * 3 + 2)
                nc.vector.tensor_tensor(qf[0:64], bank[0][0:64], cg, ALU.mult)
                dve.wait_ge(s_q3, n * 3 + 3)
                link(nc.vector.tensor_tensor(kf[0:64], bank[1][0:64], cg, ALU.mult))
                nc.vector.tensor_tensor(qf[0:64], qf[0:64], t2q[0:64], ALU.add)
                nc.vector.tensor_tensor(kf[0:64], kf[0:64], t2k[0:64], ALU.add).then_inc(s_rope, 1)
                if after_first(n):
                    dve.wait_ge(s_pexp, n)
                    link(nc.vector.reciprocal(rinv[:], rsum[:]))
                    dve.wait_ge(s_pt, n)
                dve.wait_ge(s_sc, n + 1)
                link(nc.vector.scalar_tensor_tensor(s1[:], bank[4][:].rearrange("p (a m) -> p a m", a=TB), float(P) ** -0.5,
                                                    causal.unsqueeze(1).broadcast_to([P, TB, P]), ALU.mult, ALU.add))
                link(nc.vector.tensor_reduce(nmax[:], s1[:], AX.X, ALU.max))
                nc.vector.tensor_scalar(nmax[:], nmax[:], -1.0, None, ALU.mult).then_inc(s_sm, 1)
                if after_first(n):
                    expert_rows(n - 1, 1 - par, m if par else m - 1)

            expert(0, 0, 0)
            expert(1, 1, 0)
            expert(2, 0, 1)
            expert(3, 1, 1)
            loop(2, E // 2, 8, lambda m: [expert(m * 2 + par, par, m) for par in range(2)])
            dve.wait_ge(s_pexp, E)
            dve.wait_ge(s_ys, E - 1)
            link(nc.vector.reciprocal(rinv[:], rsum[:]))
            expert_rows(E - 1, 1, E // 2 - 1)

            def split(raw, stk, par):
                nc.vector.tensor_copy(stk[0:64, par, 0], raw[0:64])
                link(nc.vector.tensor_copy(stk[64:128, par, 1], raw[64:128]))
                nc.vector.tensor_tensor(stk[64:128, par, 0], raw[0:64], stk[0:64, par, 0], ALU.subtract)
                return nc.vector.tensor_tensor(stk[0:64, par, 1], raw[64:128], stk[64:128, par, 1], ALU.subtract)

            def prep_u(g, q, par):
                dve.wait_ge(s_prep_free, prep_index(g, 1) + 1)
                if q is not None:
                    dve.wait_ge(s_f, (q - 1) * 16)
                split(u_raw, u_stk, par).then_inc(s_us, 1)

            def prep_v(g, par):
                dve.wait_ge(s_prep_free, prep_index(g, 2) + 1)
                link(split(v_raw, v_stk, par))
                nc.vector.tensor_copy(v_swp[0:64, par], v_stk[64:128, par])
                nc.vector.tensor_copy(v_swp[64:128, par], v_stk[0:64, par]).then_inc(s_vs_rdy, 1)

            def add_g(i, j):
                dve.wait_ge(s_prep_full, prep_index(i * PAIRS + j, 0) + 1)
                if j == 1:
                    ins = nc.vector.tensor_scalar(gT[:], prep_bank[:], 0.5 * FACTOR_SCALE ** 2, None, ALU.mult)
                else:
                    ins = nc.vector.scalar_tensor_tensor(gT[:], prep_bank[:], 0.5 * FACTOR_SCALE ** 2, gT[:], ALU.mult, ALU.add)
                ins.then_inc(s_prep_free, 1)

            def evac_o(g, j, o, some_before):
                dve.wait_ge(s_out, g * 8 + 4 * (o + 1))
                if some_before:
                    dve.wait_ge(s_ol, g * 2 - 1 + o)
                nc.vector.tensor_scalar(o_s[:, o], o_bank[o][:], sums[:, o, j % 2:j % 2 + 1], None, ALU.add)\
                  .then_inc(s_oe, 1)

            def parts_of_o(g, o, some_before):
                dve.wait_ge(s_oe, g * 2 + o + 1)
                if some_before:
                    dve.wait_ge(s_prep_full, prep_index(g, 0) + 1)
                nc.vector.tensor_copy(o_hl[:, o, 0], o_s[:, o]).then_inc(s_oh, 1)
                dve.wait_ge(s_oh, g * 2 + o + 1)
                nc.vector.tensor_tensor(o_hl[:, o, 1], o_s[:, o], o_hl[:, o, 0], ALU.subtract).then_inc(s_ol, 1)

            def split2(src, stk):
                link(nc.vector.tensor_copy(stk[:], src[:]))
                nc.vector.tensor_tensor(stk[64:128], src[64:128], stk[64:128], ALU.subtract).then_inc(s_stk, 1)

            def l1_statistics(L):
                wait_emptied(dve, ("back", 0), L)
                link(variances(L, mv_s))
                nc.vector.tensor_scalar(ve[:], mv_s[:, :, 1], EPS, None, ALU.add).then_inc(s_stats2, 1)

            def l1_rows(L):
                dve.wait_ge(s_rstd2, L + 1)
                normalised(xn_s, L, mv_s[:, :, 0:1], rstd_s[:].unsqueeze(2)).then_inc(s_xn2, 1)

            def l1(step, L, banks):
                kind, f = step
                s, bk = L * NL + STEP_AT[step], banks[STEP_AT[step] % len(banks)]
                if kind == "back":
                    dve.wait_ge(s_lf, s + 1)
                    nc.vector.tensor_tensor(x_all[:, L], bk[:].rearrange("p (k d) -> p k d", k=TB), x_all[:, L],
                                            ALU.add).then_inc(s_ld, 1)
                elif kind in ("k", "q"):
                    nth = L * 2 + (1 if kind == "k" else 2)
                    if kind == "k":
                        wait_emptied(dve, ("norm", 0), L)
                        nc.vector.tensor_tensor(xn2_hl[:, 1], xn2T[:], xn2_hl[:, 0], ALU.subtract).then_inc(s_x2, 1)
                    dve.wait_ge(s_lf, s + 1)
                    nc.vector.tensor_scalar(kmin[:], bk[:], 0.0, None, ALU.min).then_inc(s_min, 1)
                    dve.wait_ge(s_exp, nth)
                    nc.vector.scalar_tensor_tensor(kf32[:], bk[:], 0.0, kexp[:], ALU.max, ALU.add).then_inc(s_ld, 1)
                    wait_emptied(dve, step, L)
                    split2(kf32, k_stk if kind == "k" else q_stk)
                elif kind == "v":
                    wait_emptied(dve, step, L)
                    split2(kf32, vl_stk)
                elif kind == "A":
                    dve.wait_ge(s_lf, s + 1)
                    wait_emptied(dve, ("B", f), L)
                    nc.vector.tensor_tensor(ab[:], bk[:], (bs6 if f == NF - 1 else bs)[:], ALU.mult).then_inc(s_ld, 1)
                    wait_emptied(dve, step, L)
                    link(nc.vector.tensor_tensor_scan(pre[:], ones[:], ab[:], 0.0, ALU.mult, ALU.add))
                elif kind in "CD":
                    r, half = round_of(kind, f)
                    dve.wait_ge(s_lf, s + 1)
                    if kind == "C" and r >= 2:
                        dve.wait_ge(s_y, L * ROUNDS + r - 1)
                    nc.vector.tensor_tensor(pc[half][:, r % 2], bk[:], pre[:], ALU.mult).then_inc(s_ld, 1)
                elif kind == "den":
                    dve.wait_ge(s_lf, s + 1)
                    nc.vector.tensor_scalar(small[:, 0:TB], bk[:, 0:TB], 1e-6, None, ALU.max).then_inc(s_ld, 1)
                    wait_emptied(dve, step, L)
                    link(nc.vector.reciprocal(small[:, TB:2 * TB], small[:, 0:TB]))
                    dve.wait_ge(s_yo, L + 1)
                    for k in range(TB):
                        ins = nc.vector.scalar_tensor_tensor(x_all[:, L, k], y_bank[:, k * P:(k + 1) * P], small[:, TB + k:TB + k + 1],
                                                             x_all[:, L, k], ALU.mult, ALU.add)
                    ins.then_inc(s_yfree, 1)
                elif kind == "gate":
                    if f:
                        wait_emptied(dve, ("up", f - 1), L)
                    dve.wait_ge(s_tanh, L * HC + f + 1)
                    nc.vector.scalar_tensor_tensor(gated[:], tg[:], 1.0, bk[:], ALU.add, ALU.mult).then_inc(s_ld, 1)
                elif kind == "up":
                    dve.wait_ge(s_lf, s + 1)
                    wait_emptied(dve, ("gate", f), L)
                    nc.vector.scalar_tensor_tensor(hid[:, f], gated[:], 0.5, bk[:], ALU.mult, ALU.mult).then_inc(s_ld, 1)
                elif kind == "down":
                    dve.wait_ge(s_lf, s + 1)
                    dve.wait_ge(s_yfree, L + 1)
                    nc.vector.tensor_tensor(x_all[:, L], bk[:].rearrange("p (k d) -> p k d", k=TB), x_all[:, L],
                                            ALU.add).then_inc(s_ld, 1)

            def split_rows(batch):
                link(nc.vector.tensor_copy(xn1_hl[:, 0], xn1T[:, batch]))
                nc.vector.tensor_tensor(xn1_hl[:, 1], xn1T[:, batch], xn1_hl[:, 0], ALU.subtract).then_inc(s_x1, 1)

            def weights_back(n, par):
                mine = picks[:, n].rearrange("p (c s) -> p c s", s=NPICK)
                if later(n):
                    dve.wait_ge(s_scat, n - 1)
                nc.vector.tensor_copy(iv_s[:, par, 0], mine[:, :, 0])
                for h in range(2):
                    rows = slice(64 * h, 64 * h + 64)
                    high, low = (picks[rows, n, base:base + (E // 2 - 1) * (NPICK + 2) + 1:NPICK + 2] for base in (2 + h, 2 + E + h))
                    ins = nc.vector.tensor_tensor(iv_s[rows, par, 1], high, low, ALU.add)
                link(ins)
                for e2 in range(E // 2):
                    ins = nc.vector.tensor_scalar(selT[:, par, e2], tokens[:], iv_s[:, par, 0, e2:e2 + 1], iv_s[:, par, 1, e2:e2 + 1],
                                                  ALU.is_equal, ALU.mult)
                ins.then_inc(s_selw, 1)

            def add_experts(n, par):
                dve.wait_ge(s_scat, n + 1)
                nc.vector.tensor_tensor(x_all[:, n], bank[par][:].rearrange("p (k d) -> p k d", k=TB), x_all[:, n],
                                        ALU.add).then_inc(s_ffn, 1)
            weights_back(0, 0)
            weights_back(1, 1)

            prep_u(-1, None, 0)
            prep_v(-1, 0)
            split_rows(0)

            def add_and_weights(n, par):
                add_experts(n, par)
                weights_back(n + 2, par)
            add_and_weights(0, 0)
            add_and_weights(1, 1)
            loop(1, B // 2 - 1, 2, lambda m: [add_and_weights(m * 2 + par, par) for par in range(2)])
            add_experts(B - 2, 0)
            add_experts(B - 1, 1)

            dve.wait_ge(s_ffn, B)
            nc.vector.memset(bs6[64:128], 1.0)
            dve.wait_ge(s_parts, 6)

            def iteration(i, attn, second):
                steps = iter(L1_STEPS if second else [])
                if not attn:
                    add_g(i, 0)
                    l1(next(steps), i - 1, last_banks)
                    l1_statistics(i - 1)
                    l1_rows(i - 1)
                    for st in steps:
                        l1(st, i - 1, last_banks)
                    return
                for j in range(PAIRS):
                    g = i * 8 + j
                    for u in range(UNITS):
                        if u == TB:
                            parts_of_o(g, 0, second or j)
                        if u == 1 and (second or j):
                            add_g(i, j)
                        if second and j * UNITS + u == L1_STATS_SLOT:
                            l1_statistics(i - 1)
                        if second and j * UNITS + u == L1_ROWS_SLOT:
                            l1_rows(i - 1)
                        if second and j * UNITS + u in L1_SLOTS[:NL]:
                            l1(next(steps), i - 1, [l1_bank])
                        if u == 2:
                            prep_u(g, g + 1 if second or j else None, (j + 1) % 2)
                        if u == 3:
                            prep_v(g, (j + 1) % 2)
                        if u % TB == TB - 1:
                            evac_o(g, j, u // TB, second or j)
                            if u == UNITS - 1:
                                parts_of_o(g, 1, second or j)
                        if j == PAIRS - 1 and u == 0:
                            dve.wait_ge(s_prep_full, prep_index(g - 1, 2) + 1)
                            split_rows(i + 1)

            iteration(0, True, False)

            def body(i):
                iteration(i, True, True)
            loop(1, B, 3 * PAIRS + 1 + 2 + 3 + NF + 1, body)
            iteration(B, False, True)

        @block.scalar
        def _(act):
            def copy(dst, src):
                return nc.scalar.activation(dst, src, ACT.Copy)

            def transposed(n, par):
                act.wait_ge(s_xT, n + 1)
                copy(xn1T[:, n], bank[par][:]).then_inc(s_xnT, 1)

            def logits(n, par):
                act.wait_ge(s_lg, n + 1)
                copy(lg8[0:E, n], bank[2 + par][0:E]).then_inc(s_lgc, 1)
            lagged(fori_of(act), transposed, logits)
            act.wait_ge(s_lgd, 16)
            nc.scalar.activation(tk_work, lg[0:E * B], ACT.Exp, scale=-1.0).then_inc(s_ex, 1)
            act.wait_ge(s_tkT, 1)
            copy(rvT[:].rearrange("p a k c -> p (a k c)"), bank[2][:]).then_inc(s_rv, 1)

            def picked(n, par):
                act.wait_ge(s_gath, n + 1)
                copy(xgT[:, :, n, :], bank[par][:].rearrange("p (e q) -> p e q", e=E))
                copy(csg[:, :, n, :], bank[2 + par][:].rearrange("p (e q) -> p e q", e=E))
                copy(picks[:, n], bank[4 + par][:, 0:(E // 2) * NPICK]).then_inc(s_gx, 1)

            def high_part(n, par):
                act.wait_ge(s_xg, n + 1)
                copy(xn_hl[:, par, 0], xn_g[:, par].rearrange("p k d -> p (k d)")).then_inc(s_xgh, 1)
            lagged(fori_of(act), high_part, picked)

            def picked_rows(n):
                copy(xg_s[:], xgT[:, n].rearrange("p b q -> p (b q)")).then_inc(s_xgs, 1)

            def attended(n, first):
                act.wait_ge(s_pt, n + 1)
                if not first:
                    act.wait_ge(s_av, n)
                copy(ptT[:].rearrange("p a m -> p (a m)"), bank[5][:]).then_inc(s_ptc, 1)
                act.wait_ge(s_av, n + 1)
                if not first:
                    act.wait_ge(s_yd, n)
                copy(avT[:].rearrange("p a m -> p (a m)"), bank[6][:]).then_inc(s_avc, 1)

            def expert(n, par):
                act.wait_ge(s_q3, n * 3 + 2)
                if after_first(n):
                    act.wait_ge(s_sc, n)
                copy(qf[64:128], bank[0][64:128])
                act.wait_ge(s_q3, n * 3 + 3)
                copy(kf[64:128], bank[1][64:128]).then_inc(s_qk_hi, 1)
                if after_first(n):
                    attended(n - 1, not later(n))
                act.wait_ge(s_vd, n + 1)
                copy(v_s[:].rearrange("p a m -> p (a m)"), bank[3][:]).then_inc(s_vs, 1)
                if not (isinstance(n, int) and n == E - 1):
                    picked_rows(n + 1)
                act.wait_ge(s_sm, n + 1)
                for a in range(TB):
                    ins = nc.scalar.activation(s1[:, a], s1[:, a], ACT.Exp, bias=nmax[:, a:a + 1], accum_out=rsum[:, a:a + 1])
                ins.then_inc(s_pexp, 1)

            act.wait_ge(s_gx, B)
            picked_rows(0)
            pairs(fori_of(act), expert, 2)
            attended(E - 1, False)


            def prep_raw(g, k, raw, total, par, q):
                act.wait_ge(s_prep_full, prep_index(g, k) + 1)
                if not (isinstance(g, int) and g < 0):
                    act.wait_ge(s_us if k == 1 else s_vs_rdy, g + 1)
                    act.wait_ge(s_prep_full, 4 if isinstance(g, int) and g == 0 else prep_index(g, 0))
                if q is not None:
                    act.wait_ge(s_oe, (q - 1) * 2)
                nc.scalar.activation(raw[:], prep_bank[:], ACT.Copy, accum_out=total[:, par:par + 1]).then_inc(s_prep_free, 1)

            def prep_tok(g, k, tok, par, q):
                act.wait_ge(s_prep_full, prep_index(g, k) + 1)
                if q is not None:
                    act.wait_ge(s_out, (q - 1) * 8)
                copy(tok[:, par].rearrange("p k c -> p (k c)"), prep_bank[:]).then_inc(s_prep_free, 1)

            def tanh_unit(i, n0):
                for n in (n0, n0 + 1):
                    act.wait_ge(s_f, i * 128 + n + 1)
                    if n0 >= 4:
                        act.wait_ge(s_out, i * 64 + n0 // 2 - 1)
                    elif not isinstance(i, int):
                        act.wait_ge(s_out, i * 64 + n0 // 2 - 1)
                    nc.scalar.activation(th[:, n % TH_SLOTS], f_bank[n % F_BANKS][:], ACT.Tanh,
                                         scale=0.5 * FACTOR_SCALE ** 2).then_inc(s_th, 1)

            def l1(step, L, banks):
                kind, f = step
                s, bk = L * NL + STEP_AT[step], banks[STEP_AT[step] % len(banks)]
                if kind == "norm":
                    act.wait_ge(s_lf, s + 1)
                    copy(xn2_hl[:, 0], bk[:])
                    copy(xn2T[:], bk[:]).then_inc(s_la, 1)
                elif kind in ("k", "q"):
                    nth = L * 2 + (1 if kind == "k" else 2)
                    act.wait_ge(s_min, nth)
                    nc.scalar.activation(kexp[:], kmin[:], ACT.Exp).then_inc(s_exp, 1)
                elif kind == "v":
                    act.wait_ge(s_lf, s + 1)
                    act.wait_ge(s_stk, L * 3 + 2)
                    copy(kf32[:], bk[:]).then_inc(s_la, 1)
                elif kind == "B":
                    act.wait_ge(s_lf, s + 1)
                    if f:
                        wait_emptied(act, ("A", f - 1), L)
                    if f == NF - 1:
                        copy(bs6[0:64], bk[0:64]).then_inc(s_la, 1)
                    else:
                        copy(bs[:], bk[:]).then_inc(s_la, 1)
                elif kind == "up" and f == 0:
                    act.wait_ge(s_y, L * ROUNDS + ROUNDS)
                    copy(y_sb[:], y_bank[:]).then_inc(s_ysb, 1)
                elif kind == "gate":
                    act.wait_ge(s_lf, s + 1)
                    if f:
                        wait_emptied(act, ("gate", f - 1), L)
                    nc.scalar.activation(tg[:], bk[:], ACT.Tanh, scale=0.5).then_inc(s_tanh, 1)

            prep_raw(-1, 1, u_raw, sums[:, 1], 0, None)
            prep_raw(-1, 2, v_raw, sums[:, 0], 0, None)
            prep_tok(-1, 3, u_tok, 0, None)
            prep_tok(-1, 4, v_tok, 0, None)

            act.wait_ge(s_ffn, B)
            def iteration(i, attn, second):
                steps = iter(L1_STEPS if second else [])
                if attn:
                    tanh_unit(i, 0)
                    for j in range(PAIRS):
                        g = i * 8 + j
                        q = g + 1
                        for u in range(UNITS):
                            if j * UNITS + u < PAIRS * UNITS - 1:
                                tanh_unit(i, 2 * (j * UNITS + u + 1))
                            q1 = q if second or j else None
                            if u == 2:
                                prep_raw(g, 1, u_raw, sums[:, 1], (j + 1) % 2, q1)
                            if u == 3:
                                prep_raw(g, 2, v_raw, sums[:, 0], (j + 1) % 2, q1)
                            if u == 5:
                                prep_tok(g, 3, u_tok, (j + 1) % 2, q1)
                            if u == 6:
                                prep_tok(g, 4, v_tok, (j + 1) % 2, q1)
                            if second and j * UNITS + u in L1_SLOTS[:NL]:
                                l1(next(steps), i - 1, [l1_bank])
                else:
                    for st in steps:
                        l1(st, i - 1, last_banks)

            iteration(0, True, False)
            with act.Fori(1, B) as i:
                iteration(i, True, True)
            iteration(B, False, True)

        @block.tensor
        def _(pe):
            def mm(out, lhsT, rhs, start=True, stop=True):
                return nc.tensor.matmul(out, lhsT, rhs, start=start, stop=stop)

            pe.wait_ge(s_first, 16 * len(first_consts))
            def transposes(n, par):
                pe.wait_ge(s_xn, n + 1)
                if later(n):
                    pe.wait_ge(s_xnT, n - 1)
                for k in range(TB):
                    ins = nc.tensor.transpose(bank[par][:, k * P:(k + 1) * P], xn_g[:, par, k], ident[:])
                ins.then_inc(s_xT, 1)

            def logits(n, par):
                pe.wait_ge(s_xnT, n + 1)
                if later(n):
                    pe.wait_ge(s_lgc, n - 1)
                mm(bank[2 + par][0:E], wr_w[:], xn1T[:, n]).then_inc(s_lg, 1)
            lagged(fori_of(pe), transposes, logits)
            pe.wait_ge(s_lgc, B)
            pe.wait_ge(s_tk, 1)
            for a, src in enumerate((tk_rank, tk_val)):
                for k in range(TB):
                    ins = nc.tensor.transpose(bank[2][:, (a * TB + k) * 64:(a * TB + k + 1) * 64], src[:, k * P:(k + 1) * P],
                                              ident[0:64, 0:64])
            ins.then_inc(s_tkT, 1)
            pe.wait_ge(s_rv, 1)

            def gather(n, par):
                pe.wait_ge(s_sel, n + 1)
                if later(n):
                    pe.wait_ge(s_gx, n - 1)
                for out, parts in ((bank[par], xn_hl[:, par]), (bank[2 + par], table_hl)):
                    for k in range(TB):
                        for h in range(2):
                            mm(out[:], parts[:, h, k * P:(k + 1) * P], sels[par][:, k], k == h == 0, k == TB - 1 and h == 1)
                for e2 in range(E // 2):
                    for k in range(TB):
                        ins = mm(bank[4 + par][:, e2 * NPICK:(e2 + 1) * NPICK], sels[par][:, k, e2 * P:(e2 + 1) * P],
                                 values_hl[par][:, k], k == 0, k == TB - 1)
                ins.then_inc(s_gath, 1)
            pairs(fori_of(pe), gather)
            pe.wait_ge(s_gx, B)

            pe.wait_ge(s_const, 16 * (len(consts) + len(phase_consts)))

            def probabilities_back(n, par, m, first):
                pe.wait_ge(s_pexp, n + 1)
                if not first:
                    pe.wait_ge(s_ptc, n)
                for a in range(TB):
                    ins = nc.tensor.transpose(bank[5][:, a * P:(a + 1) * P], s1[:, a], ident[:])
                ins.then_inc(s_pt, 1)

            def attend(n, par, m, first):
                pe.wait_ge(s_ptc, n + 1)
                pe.wait_ge(s_vs, n + 1)
                if not first:
                    pe.wait_ge(s_avc, n)
                for a in range(TB):
                    ins = mm(bank[6][:, a * P:(a + 1) * P], v_s[:, a], ptT[:, a])
                ins.then_inc(s_av, 1)

            def expert_out(n, par, m, first):
                pe.wait_ge(s_avc, n + 1)
                pe.wait_ge(s_wo[par], m * 16 + 16)
                if not first:
                    pe.wait_ge(s_ys, n)
                for a in range(TB):
                    ins = mm(bank[7][:, a * P:(a + 1) * P], avT[:, a], wo_e[:, par])
                ins.then_inc(s_yd, 1)

            def expert(n, par, m):
                w = we[:, par]
                xg = xgT[:, n].rearrange("p b q -> p (b q)")
                before = (n - 1, 1 - par, m if par else m - 1, not later(n))
                pe.wait_ge(s_we[par], m * 16 + 16)
                if after_first(n):
                    pe.wait_ge(s_rope, n)
                    pe.wait_ge(s_qk_hi, n)
                mm(bank[2][:], w[:, 2 * P:3 * P], xg).then_inc(s_q3, 1)
                mm(bank[0][:], w[:, 0:P], xg).then_inc(s_q3, 1)
                mm(bank[1][:], w[:, P:2 * P], xg).then_inc(s_q3, 1)
                if after_first(n):
                    probabilities_back(*before)
                    pe.wait_ge(s_vs, n)
                pe.wait_ge(s_xgs, n + 1)
                for a in range(TB):
                    ins = mm(bank[3][:, a * P:(a + 1) * P], xg_s[:, a * P:(a + 1) * P], w[:, 3 * P:4 * P])
                ins.then_inc(s_vd, 1)
                if after_first(n):
                    attend(*before)
                pe.wait_ge(s_rope, n + 1)
                pe.wait_ge(s_qk_hi, n + 1)
                if after_first(n):
                    pe.wait_ge(s_sm, n)
                for a in range(TB):
                    ins = mm(bank[4][:, a * P:(a + 1) * P], qf[:, a * P:(a + 1) * P], kf[:, a * P:(a + 1) * P])
                ins.then_inc(s_sc, 1)
                if after_first(n):
                    expert_out(*before)

            expert(0, 0, 0)
            expert(1, 1, 0)
            with pe.Fori(1, E // 2) as m:
                for par in range(2):
                    expert(m * 2 + par, par, m)
            probabilities_back(E - 1, 1, E // 2 - 1, False)
            attend(E - 1, 1, E // 2 - 1, False)
            expert_out(E - 1, 1, E // 2 - 1, False)


            def product(bk, w_parts, cols, x_parts):
                mm(bk[:], w_parts[:, 0, cols], x_parts[:, 0], True, False)
                mm(bk[:], w_parts[:, 0, cols], x_parts[:, 1], False, False)
                return mm(bk[:], w_parts[:, 1, cols], x_parts[:, 0], False, True)

            def prep(g, k, j, batch):
                if not (isinstance(g, int) and prep_index(g, k) == 0):
                    pe.wait_ge(s_prep_free, prep_index(g, k))
                pair = slice(j * P, (j + 1) * P)
                if k in (1, 2) and isinstance(g, int) and g < 0:
                    ins = mm(prep_bank[:], (uT_w if k == 1 else vT_w)[:, pair], xn1T[:, 0])
                elif k in (1, 2):
                    if j == 0 and k == 1:
                        pe.wait_ge(s_x1, batch + 1)
                    ins = product(prep_bank, uv_hl[k - 1], pair, xn1_hl)
                else:
                    if k == 3:
                        pe.wait_ge(s_prep_free, prep_index(g, 2) + 1)
                    for t in range(TB):
                        ins = nc.tensor.transpose(prep_bank[:, t * P:(t + 1) * P], (u_raw if k == 3 else v_raw)[:, t * P:(t + 1) * P],
                                                  ident[:])
                ins.then_inc(s_prep_full, 1)

            def project(g, j):
                pe.wait_ge(s_prep_free, prep_index(g, 0))
                pe.wait_ge(s_ol, g * 2)
                was = (j - 1) % PAIRS
                passes = [(o, a, b) for o in range(2) for a, b in ((0, 0), (0, 1), (1, 0))]
                for n, (o, a, b) in enumerate(passes):
                    ins = mm(prep_bank[:], w_hl[o][:, a, was * D:(was + 1) * D], o_hl[:, o, b], n == 0, n == len(passes) - 1)
                ins.then_inc(s_prep_full, 1)

            def scores(i, un):
                j, u = un // UNITS, un % UNITS
                par, o, blk = j % 2, u // TB, u % TB
                if u == 0:
                    pe.wait_ge(s_us, i * PAIRS + j + 1)
                    pe.wait_ge(s_vs_rdy, i * PAIRS + j + 1)
                for h in range(2):
                    n = 2 * un + h
                    if n >= F_BANKS:
                        pe.wait_ge(s_th, i * 128 + n - F_BANKS + 1)
                    elif not isinstance(i, int):
                        pe.wait_ge(s_th, i * 128 - (1, 0, 2)[n])
                    bk = f_bank[n % F_BANKS]
                    cols = slice(blk * P, (blk + 1) * P)
                    if o == 0:
                        mm(bk[:], v_stk[:, par, h, cols], u_stk[:, par, h], True, False)
                        ins = mm(bk[:], v_swp[:, par, h, cols], u_stk[:, par, h], False, True)
                    else:
                        mm(bk[:], u_stk[:, par, h, cols], v_stk[:, par, h], True, False)
                        ins = mm(bk[:], u_stk[:, par, h, cols], v_swp[:, par, h], False, True)
                    ins.then_inc(s_f, 1)

            def weighted(i, un, first_batch):
                j, u = un // UNITS, un % UNITS
                par, o, blk = j % 2, u // TB, u % TB
                g = i * PAIRS + j
                if u == 0:
                    pe.wait_ge(s_prep_free, 4 if first_batch and j == 0 else prep_index(g - 1, 4) + 1)
                if blk == 0 and not (first_batch and j == 0):
                    pe.wait_ge(s_oe, g * 2 - 1 + o)
                pe.wait_ge(s_th, i * 128 + 2 * un + 2)
                tok = (v_tok, u_tok)[o]
                for h in range(2):
                    rows = slice(64 * h, 64 * h + 64)
                    ins = mm(o_bank[o][rows], tok[:, par, blk, rows], th[:, (2 * un + h) % TH_SLOTS], blk == 0, blk == TB - 1)
                ins.then_inc(s_out, 1)

            def spread(bk, step, f):
                at0 = E_AT[step] + f * P
                src = {"A": k_stk, "B": vl_stk, "C": q_stk, "D": q_stk}[step]
                ins = mm(bk[:], e_str[:, at0:at0 + P], src[:], True, f < 2)
                if f >= 2:
                    ins = mm(bk[:], e_swp[:, at0:at0 + P], src[:], False, True)
                return ins

            def y_round(r, L):
                wait_emptied(pe, ("C", 1) if r == 0 else ("D", r + 1), L)
                mm(y_bank[0:64], top_w[:, r], pc[0][:, r % 2], r == 0, r == ROUNDS - 1)
                mm(y_bank[64:128], bot_w[:, r], pc[1][:, r % 2], r == 0, r == ROUNDS - 1).then_inc(s_y, 1)

            def l1(step, L, banks):
                kind, f = step
                at, bk = STEP_AT[step], banks[STEP_AT[step] % len(banks)]
                if kind == "C" and f >= 2:
                    y_round(f - 2, L)
                if kind == "gate" and f == 0:
                    y_round(ROUNDS - 1, L)
                if kind == "norm":
                    pe.wait_ge(s_xn2, L + 1)
                if kind == "B" and f == 0:
                    pe.wait_ge(s_stk, L * 3 + 3)
                if kind == "k":
                    wait_emptied(pe, ("norm", 0), L)
                if kind == "down":
                    wait_emptied(pe, ("up", HC - 1), L)
                if at >= len(banks):
                    wait_emptied(pe, L1_STEPS[at - len(banks)], L)
                if kind == "back":
                    pe.wait_ge(s_prep_free, prep_index((L + 1) * PAIRS, 0) + 1)
                    for t in range(TB):
                        ins = nc.tensor.transpose(bk[:, t * P:(t + 1) * P], gT[:, t * P:(t + 1) * P], ident[:])
                elif kind == "norm":
                    for t in range(TB):
                        ins = nc.tensor.transpose(bk[:, t * P:(t + 1) * P], xn_s[:, t], ident[:])
                elif kind in ("k", "q", "v"):
                    ins = mm(bk[:], {"k": kk_w, "q": qq_w, "v": vv_w}[kind][:], xn2T[:])
                elif kind in ("A", "B", "C", "D"):
                    ins = spread(bk, kind, f)
                elif kind == "den":
                    for t in range(TB):
                        ins = mm(bk[:, t:t + 1], pc[0][:, (ROUNDS - 1) % 2, t * P:(t + 1) * P], zsel[:])
                elif kind in ("gate", "up"):
                    if kind == "gate" and f == 0:
                        pe.wait_ge(s_x2, L + 1)
                    ins = product(bk, gu_hl[kind == "up"], slice(f * P, (f + 1) * P), xn2_hl)
                elif kind == "down":
                    for t in range(TB):
                        for h in range(HC):
                            ins = mm(bk[:, t * P:(t + 1) * P], hid[:, h, t * P:(t + 1) * P], wd[:, h], h == 0, h == HC - 1)
                ins.then_inc(s_lf, 1)
                if kind == "den":
                    pe.wait_ge(s_ysb, L + 1)
                    for t in range(TB):
                        ins = mm(y_bank[:, t * P:(t + 1) * P], y_sb[:, t * P:(t + 1) * P], wo2[:])
                    ins.then_inc(s_yo, 1)

            for k in range(1, 5):
                prep(-1, k, 0, 0)

            pe.wait_ge(s_ymv[0], 16 * E)
            pe.wait_ge(s_ymv[1], 16 * E)

            def scatter(n, par):
                pe.wait_ge(s_selw, n + 1)
                if later(n):
                    pe.wait_ge(s_ffn, n - 1)
                for k in range(TB):
                    for e2 in range(E // 2):
                        ins = mm(bank[par][:, k * P:(k + 1) * P], selT[:, par, e2, k * P:(k + 1) * P], y_all[:, n, e2],
                                 e2 == 0, e2 == E // 2 - 1)
                ins.then_inc(s_scat, 1)
            pairs(fori_of(pe), scatter)

            pe.wait_ge(s_ffn, B)
            pe.wait_ge(s_prep_w, 1)
            pe.wait_ge(s_ones, 2)
            def iteration(i, attn, second):
                steps = iter(L1_STEPS if second else [])
                if not attn:
                    project(i * PAIRS, 0)
                    pe.wait_ge(s_prep_free, prep_index(i * PAIRS, 0) + 1)
                    for st in steps:
                        l1(st, i - 1, last_banks)
                    return
                scores(i, 0)
                for j in range(PAIRS):
                    g = i * PAIRS + j
                    for u in range(UNITS):
                        un = j * UNITS + u
                        if un < PAIRS * UNITS - 1:
                            scores(i, un + 1)
                        weighted(i, un, not second)
                        if u == 1 and (second or j):
                            project(g, j)
                        if u in (2, 3, 5, 6):
                            prep(g, {2: 1, 3: 2, 5: 3, 6: 4}[u], (j + 1) % PAIRS, i if j < PAIRS - 1 else i + 1)
                        if second and un in L1_SLOTS[:NL]:
                            l1(next(steps), i - 1, [l1_bank])

            pe.wait_ge(s_parts, 6)
            pe.wait_ge(s_x1, 1)
            iteration(0, True, False)
            with pe.Fori(1, B) as i:
                iteration(i, True, True)
            iteration(B, False, True)


def tables():
    half = NROT // 2
    inv = (np.float32(1.0) / np.float32(10000.0) ** (np.arange(half, dtype=np.float32) * np.float32(2.0) / np.float32(NROT))).astype(np.float32)
    ang = np.arange(T, dtype=np.float32)[:, None] * inv
    cos, sin = np.cos(ang).astype(np.float32), np.sin(ang).astype(np.float32)
    at = np.arange(P)
    same = at[:, None] // KSEL == at[None, :] // KSEL
    seen = same & (at[:, None] >= at[None, :])
    return {
        "table": np.concatenate([cos, cos, -sin, sin], axis=1),
        "causal": np.where(seen, 0.0, MASKED).astype(np.float32),
        "ident": np.eye(P, dtype=np.float32),
        "tokens": np.tile(np.arange(T, dtype=np.float32), (P, 1)),
        "token_at": (np.arange(TB)[None, :] * P + at[:, None]).astype(np.float32),
        "iota1": np.tile(np.arange(1, KSEL + 1, dtype=np.float32), (P, 1)),
        "zsel": (at >= 64).astype(np.float32)[:, None],
    }


def laid_out(x):
    f32 = np.float32
    wqkv, wo = x["L0_ffn_Wqkv"], x["L0_ffn_Wo"]
    turned = np.concatenate([np.arange(32, 64), np.arange(32)])
    wq, wk, wv = wqkv[:, :, 0:P], wqkv[:, :, P:2 * P], wqkv[:, :, 2 * P:]
    we = np.concatenate([wq, wk, wq[:, :, turned], wk[:, :, turned], wv, wo], axis=2)

    eye = np.eye(DH, dtype=f32)
    ea, eb, ed = (np.zeros((DH, NF * P), f32) for _ in range(3))
    top, bot = (np.zeros((NF * P, DH), f32) for _ in range(2))
    f = 0
    for n in range(DH // LEAF):
        for i in range(LEAF):
            for j in range(LEAF):
                ea[:, f], eb[:, f] = eye[:, n * LEAF + i], eye[:, n * LEAF + j]
                top[f] = eye[n * LEAF + i]
                f += 1
    for lv, (bs, r, nodes) in enumerate(LEVELS):
        UL, VR, UR, VL = (x[f"L1_attn_{w}{lv}"] for w in ("UL", "VR", "UR", "VL"))
        for n in range(nodes):
            left = slice(2 * bs * n, 2 * bs * n + bs)
            right = slice(2 * bs * n + bs, 2 * bs * (n + 1))
            for i in range(r):
                for j in range(r):
                    ea[left, f], eb[right, f], ed[left, f] = UL[:, i], VR[:, j], VL[:, i]
                    top[f, left], bot[f, right] = UL[:, i], UR[:, j]
                    f += 1
    ea[:, f:f + DH] = eb[:, f:f + DH] = eye
    assert f + DH == NF * P
    e = np.concatenate([ea, eb, ed[:, 2 * P:]], axis=1)
    tiles = lambda a: a.reshape(NF, P, DH)
    top_w = np.stack([tiles(top)[t] for t in (0, 2, 3, 4, 5, 6)], axis=1)
    bot_w = np.stack([tiles(top)[1]] + [tiles(bot)[t] for t in (2, 3, 4, 5, 6)], axis=1)
    twice = lambda w: np.concatenate([w, w], axis=1)
    wd = x["L1_ffn_w_down"].T.reshape(HC, P, D).transpose(1, 0, 2).reshape(P, HIDDEN)
    return {
        "x": x["L0_attn_qz"],
        "u": x["L0_attn_ternary_factor_u"], "v": x["L0_attn_ternary_factor_v"],
        "uT": x["L0_attn_ternary_factor_u"].T, "vT": x["L0_attn_ternary_factor_v"].T,
        "wrT": x["L0_ffn_Wr"].T, "we": we,
        "wk2": twice(x["L1_attn_Wk"]), "wq2": twice(x["L1_attn_Wq"]), "wv2": twice(x["L1_attn_Wv"]),
        "wo2": np.concatenate([x["L1_attn_Wo"]] * 2, axis=0),
        "top": top_w, "bot": bot_w, "e": np.concatenate([e, e], axis=0),
        "wi": np.stack([x["L1_ffn_w_gate"].T, x["L1_ffn_w_up"].T, wd], axis=1),
    }


def kernel(**inputs):
    import concourse.bacc as bacc
    from concourse.bass_utils import run_bass_kernel_spmd

    nc = bacc.Bacc("TRN2", target_bir_lowering=False, num_devices=1)
    arrays, io = {}, {}
    for name, a in {**laid_out({k: np.asarray(v) for k, v in inputs.items()}), **tables()}.items():
        a = np.ascontiguousarray(a)
        arrays[f"in_{name}"] = a
        io[name] = nc.dram_tensor(f"in_{name}", a.shape, mybir.dt.from_np(a.dtype), kind="ExternalInput").ap()
    io["out"] = nc.dram_tensor("out_0", (B, T, D), F32, kind="ExternalOutput").ap()
    build(nc, io)
    return run_bass_kernel_spmd(nc, [arrays], core_ids=[0]).results[0]["out_0"]
```
